# Optimizing a Trainium2 kernel written in Bass

```python
import numpy as np
import jax
import jax.numpy as jnp

def _softmax(x, axis=-1):
    return jax.nn.softmax(x, axis=axis)

def _gelu(x):
    return jax.nn.gelu(x, approximate=True)

def _silu(x):
    return jax.nn.silu(x)

def _sigmoid(x):
    return jax.nn.sigmoid(x)

def _layernorm(x, axis=-1, eps=1e-05):
    m = jnp.mean(x, axis=axis, keepdims=True)
    v = jnp.var(x, axis=axis, keepdims=True)
    return (x - m) / jnp.sqrt(v + eps)

def _scatter_add(tgt, idx, src, axis=0):
    return tgt.at[idx].add(src)

def _segment_sum(src, seg, n):
    return jax.ops.segment_sum(src, seg, n)
kernel_name = 'mk_seq_postln_d2_jaxref_r8_17c5dd'

def setup_inputs(seed: int=0):
    np.random.seed(seed)
    _w = jnp.asarray

    def _L0_attn_setup():
        import jax, jax.numpy as jnp
        import numpy as np
        D_MODEL = 128
        Q_HEADS = 16
        KV_HEADS = 4
        HEAD_DIM = D_MODEL // Q_HEADS
        KV_DIM = HEAD_DIM * KV_HEADS
        GROUPS = Q_HEADS // KV_HEADS
        LN_EPS = 1e-05
        NEG_INF = -10000000000.0
        key = jax.random.key(seed)
        ks = jax.random.split(key, 6)
        b, n = (2, 256)

        def xavier(k, fan_in, fan_out):
            limit = np.sqrt(6.0 / (fan_in + fan_out)).astype(np.float32)
            return jax.random.uniform(k, (fan_in, fan_out), jnp.float32, -limit, limit)
        return {'x': jax.random.normal(ks[0], (b, n, D_MODEL), jnp.float32), 'Wq': xavier(ks[1], D_MODEL, D_MODEL), 'bq': jnp.zeros((D_MODEL,), jnp.float32), 'Wk': xavier(ks[2], D_MODEL, KV_DIM), 'bk': jnp.zeros((KV_DIM,), jnp.float32), 'Wv': xavier(ks[3], D_MODEL, KV_DIM), 'bv': jnp.zeros((KV_DIM,), jnp.float32), 'ln_g': jnp.ones((D_MODEL,), jnp.float32), 'ln_b': jnp.zeros((D_MODEL,), jnp.float32), 'Wo': xavier(ks[4], D_MODEL, D_MODEL), 'bo': jnp.zeros((D_MODEL,), jnp.float32)}
    _L0_attn_in = _L0_attn_setup()

    def _L0_ffn_setup():
        import jax, jax.numpy as jnp
        import numpy as np
        B, S, D = (2, 256, 128)
        E, H, K = (8, 704, 2)
        N_RESERVED = 4
        key = jax.random.key(seed)
        ks = jax.random.split(key, 5)
        scale = 0.02
        x = jax.random.normal(ks[0], (B, S, D), dtype=jnp.float32)
        gate_w = jax.random.normal(ks[1], (E, D), dtype=jnp.float32) * scale
        w1 = jax.random.normal(ks[2], (E, D, H), dtype=jnp.float32) * scale
        w3 = jax.random.normal(ks[3], (E, D, H), dtype=jnp.float32) * scale
        w2 = jax.random.normal(ks[4], (E, H, D), dtype=jnp.float32) * scale
        return {'x': x, 'gate_w': gate_w, 'w1': w1, 'w2': w2, 'w3': w3}
    _L0_ffn_in = _L0_ffn_setup()

    def _L1_attn_setup():
        import jax, jax.numpy as jnp
        import numpy as np
        import math
        D_MODEL = 128
        D_QUERY = 64
        key = jax.random.key(seed)
        k1, k2, k3, k4 = jax.random.split(key, 4)
        X = jax.random.normal(k1, (4, 512, D_MODEL), dtype=jnp.float32)
        Wq = jax.random.normal(k2, (D_MODEL, D_QUERY), dtype=jnp.float32) * (1.0 / math.sqrt(D_MODEL))
        Wk = jax.random.normal(k3, (D_MODEL, D_QUERY), dtype=jnp.float32) * (1.0 / math.sqrt(D_MODEL))
        Wv = jax.random.normal(k4, (D_MODEL, D_MODEL), dtype=jnp.float32) * (1.0 / math.sqrt(D_MODEL))
        return {'X': X, 'Wq': Wq, 'Wk': Wk, 'Wv': Wv}
    _L1_attn_in = _L1_attn_setup()

    def _L1_ffn_setup():
        import jax, jax.numpy as jnp
        import numpy as np
        B, S, D_MODEL, D_FF = (4, 256, 128, 512)

        def _quantum_transform(hidden, theta, w_real, w_imag):
            imag = w_imag * jnp.sin(theta + hidden * 0.1)
            quantum_phase = jnp.cos(theta) * w_real + jnp.sin(theta) * w_imag
            return hidden + quantum_phase * imag * 0.1
        key = jax.random.key(seed)
        ks = jax.random.split(key, 8)
        return {'x': jax.random.normal(ks[0], (B, S, D_MODEL), dtype=jnp.float32), 'W1': jax.random.normal(ks[1], (D_MODEL, D_FF), dtype=jnp.float32) * (1.0 / np.sqrt(D_MODEL)), 'b1': jnp.zeros((D_FF,), dtype=jnp.float32), 'quantum_phases': jax.random.normal(ks[2], (D_FF,), dtype=jnp.float32) * (2.0 * np.pi), 'quantum_weights_real': jax.random.normal(ks[3], (D_FF,), dtype=jnp.float32) * 0.1, 'quantum_weights_imag': jax.random.normal(ks[4], (D_FF,), dtype=jnp.float32) * 0.1, 'W2': jax.random.normal(ks[5], (D_FF, D_MODEL), dtype=jnp.float32) * (1.0 / np.sqrt(D_FF)), 'b2': jnp.zeros((D_MODEL,), dtype=jnp.float32)}
    _L1_ffn_in = _L1_ffn_setup()
    _d = {'L0_attn_x': _L0_attn_in['x'], 'L0_attn_Wq': _L0_attn_in['Wq'], 'L0_attn_bq': _L0_attn_in['bq'], 'L0_attn_Wk': _L0_attn_in['Wk'], 'L0_attn_bk': _L0_attn_in['bk'], 'L0_attn_Wv': _L0_attn_in['Wv'], 'L0_attn_bv': _L0_attn_in['bv'], 'L0_attn_ln_g': _L0_attn_in['ln_g'], 'L0_attn_ln_b': _L0_attn_in['ln_b'], 'L0_attn_Wo': _L0_attn_in['Wo'], 'L0_attn_bo': _L0_attn_in['bo'], 'L0_ffn_gate_w': _L0_ffn_in['gate_w'], 'L0_ffn_w1': _L0_ffn_in['w1'], 'L0_ffn_w2': _L0_ffn_in['w2'], 'L0_ffn_w3': _L0_ffn_in['w3'], 'L1_attn_Wq': _L1_attn_in['Wq'], 'L1_attn_Wk': _L1_attn_in['Wk'], 'L1_attn_Wv': _L1_attn_in['Wv'], 'L1_ffn_W1': _L1_ffn_in['W1'], 'L1_ffn_b1': _L1_ffn_in['b1'], 'L1_ffn_quantum_phases': _L1_ffn_in['quantum_phases'], 'L1_ffn_quantum_weights_real': _L1_ffn_in['quantum_weights_real'], 'L1_ffn_quantum_weights_imag': _L1_ffn_in['quantum_weights_imag'], 'L1_ffn_W2': _L1_ffn_in['W2'], 'L1_ffn_b2': _L1_ffn_in['b2']}
    _x0 = _d['L0_attn_x']
    _d['L0_attn_x'] = jax.random.normal(jax.random.fold_in(jax.random.key(seed), 1), (4, 512, 128), dtype=_x0.dtype)
    del _x0
    return _d

def reference(L0_attn_x, L0_attn_Wq, L0_attn_bq, L0_attn_Wk, L0_attn_bk, L0_attn_Wv, L0_attn_bv, L0_attn_ln_g, L0_attn_ln_b, L0_attn_Wo, L0_attn_bo, L0_ffn_gate_w, L0_ffn_w1, L0_ffn_w2, L0_ffn_w3, L1_attn_Wq, L1_attn_Wk, L1_attn_Wv, L1_ffn_W1, L1_ffn_b1, L1_ffn_quantum_phases, L1_ffn_quantum_weights_real, L1_ffn_quantum_weights_imag, L1_ffn_W2, L1_ffn_b2):

    def _L0_attn_ref(x, Wq, bq, Wk, bk, Wv, bv, ln_g, ln_b, Wo, bo):
        import jax, jax.numpy as jnp
        import numpy as np
        D_MODEL = 128
        Q_HEADS = 16
        KV_HEADS = 4
        HEAD_DIM = D_MODEL // Q_HEADS
        KV_DIM = HEAD_DIM * KV_HEADS
        GROUPS = Q_HEADS // KV_HEADS
        LN_EPS = 1e-05
        NEG_INF = -10000000000.0
        b, n, _ = x.shape
        q = x @ Wq + bq
        k = x @ Wk + bk
        v = x @ Wv + bv
        q = q.reshape(b, n, GROUPS, KV_HEADS, HEAD_DIM)
        q = jnp.transpose(q, (0, 2, 3, 1, 4))
        k = k.reshape(b, n, KV_HEADS, HEAD_DIM)
        v = v.reshape(b, n, KV_HEADS, HEAD_DIM)
        scale = jnp.asarray(HEAD_DIM ** 0.5, q.dtype)
        q = q / scale
        attn_logits = jnp.einsum('bghnd,bmhd->bghnm', q, k)
        causal = jnp.tril(jnp.ones((n, n), dtype=bool))
        attn_logits = jnp.where(causal[None, None, None, :, :], attn_logits, NEG_INF)
        attn = jax.nn.softmax(attn_logits, axis=-1)
        out = jnp.einsum('bghnm,bmhd->bghnd', attn, v)
        out = jnp.transpose(out, (0, 3, 1, 2, 4)).reshape(b, n, D_MODEL)
        mu = jnp.mean(out, axis=-1, keepdims=True)
        var = jnp.var(out, axis=-1, keepdims=True)
        out = (out - mu) * jax.lax.rsqrt(var + LN_EPS) * ln_g + ln_b
        out = out @ Wo + bo
        return out

    def _L0_ffn_ref(x, gate_w, w1, w2, w3):
        import jax, jax.numpy as jnp
        import numpy as np
        B, S, D = (2, 256, 128)
        E, H, K = (8, 704, 2)
        N_RESERVED = 4
        b, s, d = x.shape
        T = b * s
        xf = x.reshape(T, d)
        logits = xf @ gate_w.T
        expert_ids = jnp.arange(E)
        logits = jnp.where(expert_ids[None, :] >= E - N_RESERVED, -jnp.inf, logits)
        weights = jax.nn.softmax(logits, axis=-1)
        top_w, top_idx = jax.lax.top_k(weights, K)
        top_w = top_w / jnp.sum(top_w, axis=-1, keepdims=True)
        cw = jnp.zeros((T, E), dtype=x.dtype).at[jnp.arange(T)[:, None], top_idx].add(top_w)
        h = jax.nn.silu(jnp.einsum('td,edh->teh', xf, w1)) * jnp.einsum('td,edh->teh', xf, w3)
        y = jnp.einsum('teh,ehd->ted', h, w2)
        out = jnp.einsum('te,ted->td', cw, y)
        return out.reshape(b, s, d)

    def _L1_attn_ref(X, Wq, Wk, Wv):
        import jax, jax.numpy as jnp
        import numpy as np
        import math
        D_MODEL = 128
        D_QUERY = 64
        B, T, _ = X.shape
        Q = X @ Wq
        K = X @ Wk
        V = X @ Wv
        scores = jnp.einsum('btd,bsd->bts', Q, K)
        causal = jnp.tril(jnp.ones((T, T), dtype=bool))
        scores = jnp.where(causal[None, :, :], scores, -jnp.inf)
        attn = jax.nn.softmax(scores / math.sqrt(D_QUERY), axis=2)
        return attn @ V

    def _L1_ffn_ref(x, W1, b1, quantum_phases, quantum_weights_real, quantum_weights_imag, W2, b2):
        import jax, jax.numpy as jnp
        import numpy as np
        B, S, D_MODEL, D_FF = (4, 256, 128, 512)

        def _quantum_transform(hidden, theta, w_real, w_imag):
            imag = w_imag * jnp.sin(theta + hidden * 0.1)
            quantum_phase = jnp.cos(theta) * w_real + jnp.sin(theta) * w_imag
            return hidden + quantum_phase * imag * 0.1
        hidden = jnp.einsum('bsd,df->bsf', x, W1) + b1
        q = _quantum_transform(hidden, quantum_phases, quantum_weights_real, quantum_weights_imag)
        act = jax.nn.relu(q)
        return jnp.einsum('bsf,fd->bsd', act, W2) + b2
    x = L0_attn_x
    x = _layernorm(x + _L0_attn_ref(x, L0_attn_Wq, L0_attn_bq, L0_attn_Wk, L0_attn_bk, L0_attn_Wv, L0_attn_bv, L0_attn_ln_g, L0_attn_ln_b, L0_attn_Wo, L0_attn_bo), axis=-1)
    x = _layernorm(x + _L0_ffn_ref(x, L0_ffn_gate_w, L0_ffn_w1, L0_ffn_w2, L0_ffn_w3), axis=-1)
    x = _layernorm(x + _L1_attn_ref(x, L1_attn_Wq, L1_attn_Wk, L1_attn_Wv), axis=-1)
    x = _layernorm(x + _L1_ffn_ref(x, L1_ffn_W1, L1_ffn_b1, L1_ffn_quantum_phases, L1_ffn_quantum_weights_real, L1_ffn_quantum_weights_imag, L1_ffn_W2, L1_ffn_b2), axis=-1)
    return x

_drawn_inputs = setup_inputs


def setup_inputs(seed=0):
    import zlib

    import numpy as np

    out = dict(_drawn_inputs(seed))
    spreads = {'L0_attn_bq': (0.0, 0.1),
     'L0_attn_bk': (0.0, 2.0),
     'L0_attn_bv': (0.0, 0.1),
     'L0_attn_ln_g': (1.0, 0.2),
     'L0_attn_ln_b': (0.0, 0.1),
     'L0_attn_bo': (0.0, 0.1),
     'L1_ffn_b1': (0.0, 0.1),
     'L1_ffn_b2': (0.0, 0.1)}
    factors = {'L0_ffn_gate_w': 8.0,
     'L0_ffn_w1': 6.137,
     'L0_ffn_w2': 6.175,
     'L0_ffn_w3': 6.101,
     'L1_ffn_quantum_phases': 8.0,
     'L1_ffn_quantum_weights_real': 34.26,
     'L1_ffn_quantum_weights_imag': 8.0}
    for name, (base, spread) in spreads.items():
        noise = np.random.default_rng([zlib.crc32(name.encode()), seed]).standard_normal(out[name].shape)
        drawn = base * np.exp(spread * noise) if base else spread * noise
        out[name] = jnp.asarray(drawn.astype(out[name].dtype))
    for name, factor in factors.items():
        out[name] = (out[name] * factor).astype(out[name].dtype)
    return out
```

```python
from contextlib import ExitStack

import numpy as np

import concourse.bass as bass
from concourse import mybir

FP32 = mybir.dt.float32
FP32R = mybir.dt.float32r
BF16 = mybir.dt.bfloat16
I32 = mybir.dt.int32
ALU = mybir.AluOpType
ACT = mybir.ActivationFunctionType
AX = mybir.AxisListType

P = 128
B, S, D = 4, 512, 128
NT = S // P
H, G, HD = 4, 4, 8
NH = H * G
KV = H * HD
PARTS = 3
TERMS = PARTS * PARTS
ROWS = 96
E, FF0 = 4, 704
FULL = FF0 // P
TAIL = FF0 - FULL * P
NM = E * FF0 // P
DQ = 64
FF1 = 512
NF = FF1 // P
EPS = 1e-5
NEG = -1e30
SCALE0 = float(HD) ** -0.5
SCALE1 = float(DQ) ** -0.5
TWO_PI = 2.0 * np.pi
PI_C1 = 6.28125
PI_C2 = float(np.float32(TWO_PI - PI_C1))
TURN = float(np.nextafter(np.float32(TWO_PI), np.float32(0)))
ROUND = 1.5 * 2.0 ** 23
RSQRT_SEED = float(0x5F3759DF)

MAX_GROUPS = [(qt, h0, hn) for qt, hn in ((0, 4), (1, 2), (2, 1), (3, 1)) for h0 in range(0, NH, hn)]
UNITS = [[(0, h, 0, 0), (3, h, 512, 384), (1, h, 640, 128)] for h in range(H)]
UNITS.append([(2, h, 256 * h, 256) for h in range(H)])
NU = len(UNITS)
PLACE = {(kb, h): (u, col, q0) for u, unit in enumerate(UNITS) for kb, h, col, q0 in unit}
EXPERT_TILES = [[FULL * e + j for j in range(FULL)] + [E * FULL + e // 2] for e in range(E)]


W_TURNS = 10
N_FRONT = 51
N_BACK = 73
N_VEC = 4 * NF + E + 4


def tiles_of(dst, src):
    pairs = [(dst[:, 0:E * FULL, :].rearrange("p (e n) c -> p e (n c)", e=E), src[:, :, 0:FULL * P])]
    for m in range(E // 2):
        pairs.append((dst[:, E * FULL + m, :].rearrange("p (e c) -> p e c", e=2),
                      src[:, 2 * m:2 * m + 2, FULL * P:FF0]))
    return pairs


class Chain:

    def __init__(self, eng, sem, per):
        self.eng, self.sem, self.per = eng, sem, per

    def begin(self, b):
        self.base, self.n = b * self.per, 0

    def link(self, ins):
        self.n += 1
        ins.then_inc(self.sem, 1)
        self.eng.wait_ge(self.sem, self.base + self.n)

    def end(self):
        assert self.n == self.per, (self.n, self.per)


def build(nc, x, Wq0, bq0, Wk0, bk0, Wv0, bv0, ln_g, ln_b, Wo0, bo0, gate_w, w1, w2, w3,
          Wq1, Wk1, Wv1, fW1, fb1, theta, w_real, w_imag, fW2, fb2, out):
    ctx = ExitStack()
    with ctx:
        def sb(name, shape, dt=FP32):
            return ctx.enter_context(nc.sbuf_tensor(name, shape, dt))

        def sem(name):
            return ctx.enter_context(nc.semaphore(name))

        ident = sb("ident", [P, P])
        ident_h = sb("ident_h", [P, P], BF16)
        future_h = sb("future_h", [P, 4, P], BF16)
        before = sb("before", [P, E, E])
        wq0 = sb("wq0", [P, D])
        wk0 = sb("wk0", [P, KV])
        wv0 = sb("wv0", [P, KV])
        wo0 = sb("wo0", [P, D])
        vec_rows = sb("vec_rows", [N_VEC, P])
        vecs = sb("vecs", [P, N_VEC])
        theta_c, w_real_c, w_imag_c, fb1_c = (vecs[:, NF * n:NF * (n + 1)] for n in range(4))
        gateT = vecs[:, 4 * NF:4 * NF + E]
        bq_c, lng_c, lnb_c, bk_c = (vecs[:, 4 * NF + E + n:4 * NF + E + n + 1] for n in range(4))
        bv_r = sb("bv_r", [P, KV])
        bo_r = sb("bo_r", [P, D])
        b2_r = sb("b2_r", [P, D])
        up_hi = [sb(f"up{n}_hi", [P, NM, P], FP32R) for n in range(2)]
        up_lo = [sb(f"up{n}_lo", [P, NM, P], FP32R) for n in range(2)]
        down = sb("down", [P, E * (FULL + 1), D])
        wq1 = sb("wq1", [P, 2, DQ])
        wk1 = sb("wk1", [P, 2, DQ])
        wv1 = sb("wv1", [P, D])
        f1 = sb("f1", [P, FF1])
        f1_hi = sb("f1_hi", [P, FF1], FP32R)
        f1_lo = sb("f1_lo", [P, FF1], FP32R)
        f2 = sb("f2", [P, NF, D])
        th = sb("th", [P, 8, NF])
        xin = sb("xin", [P, NT, D])
        xres = sb("xres", [P, NT, D])
        xT = sb("xT", [P, S])
        part_f = sb("part_f", [P, S])
        zT = part_f
        qparts = sb("qparts", [P, PARTS, S], BF16)
        kparts = sb("kparts", [KV, PARTS, S], BF16)
        qstack = sb("qstack", [P, NH, S], BF16)
        kstack = sb("kstack", [P, H, S], BF16)
        vext = sb("vext", [P, NT, H, 32])
        negmax = sb("negmax", [P, NT, NH])
        mrow = sb("mrow", [NH, S])
        mparts = sb("mparts", [NH, PARTS, S], BF16)
        hidT = sb("hidT", [P, NM, S])
        flat = hidT[:].rearrange("p a b -> p (a b)")
        probs = flat[:, 0:2 * NU * 1024].rearrange("p (a u n) -> p a u n", a=2, u=NU)
        stage = flat[:, 0:2 * E * FF0].rearrange("p (w e n) -> p w e n", w=2, e=E)
        uT = sb("uT", [P, G, S])
        rden0 = sb("rden0", [P, NT, NH])
        att = sb("att", [P, NT, D])
        attn = xT[:].rearrange("p (t d) -> p t d", t=NT)
        res1 = att
        x1 = sb("x1", [P, NT, D])
        x1T = sb("x1T", [P, S])
        x1_hi = sb("x1_hi", [P, S], FP32R)
        x1_lo = sb("x1_lo", [P, S], FP32R)
        lg = sb("lg", [P, NT, E])
        lgx = sb("lgx", [P, 3, NT, E])
        cmp4 = sb("cmp4", [P, 2, NT, E, E])
        lgs = sb("lgs", [P, 3, NT])
        cw = sb("cw", [P, NT, E])
        silu = sb("silu", [P, 2, S])
        res = sb("res", [P, NT, D])
        x2 = sb("x2", [P, NT, D])
        two_a = sb("two_a", [P, 2, S])
        x2T = two_a[:, 0, :]
        v1 = two_a[:, 1, :].rearrange("p (t d) -> p t d", t=NT)
        hid1 = two_a
        two_b = sb("two_b", [P, 2, S])
        prob1 = two_b[:, 0, :]
        probT1 = two_b[:, 1, :]
        ang = two_b
        ang_n = sb("ang_n", [P, S])
        q1 = sb("q1", [P, S], FP32R)
        k1a = sb("k1a", [P, S], FP32R)
        k1b = sb("k1b", [P, S], FP32R)
        x3_hi, x3_lo = q1, k1a
        nmax1 = sb("nmax1", [P, 2, NT])
        den1 = sb("den1", [P, 2, NT])
        x3 = sb("x3", [P, NT, D])
        actT = uT
        y = sb("y", [P, NT, D])
        carry = sb("carry", [P, 1 + G * NU])
        stats = [sb(f"stats{n}", [P, NT, 6]) for n in range(2)]
        mv = [sb(f"mv{n}", [P, NT, 2]) for n in range(2)]
        ln_s = [sb(f"ln_s{n}", [P, 4, NT]) for n in range(2)]

        ps = ctx.enter_context(nc.psum_tensor("ps", [P, 8, 512], FP32))
        q_scr = nc.dram_tensor("q_scr", (PARTS, D, S), BF16, kind="Internal").ap()
        k_scr = nc.dram_tensor("k_scr", (PARTS, KV, S), BF16, kind="Internal").ap()
        m_scr = nc.dram_tensor("m_scr", (PARTS, NH, S), BF16, kind="Internal").ap()

        w_in = sem("w_in")
        w_up_in = sem("w_up_in")
        w_down_in = sem("w_down_in")
        w_pool = sem("w_pool")
        w_zero = sem("w_zero")
        w_dve = sem("w_dve")
        w_act = sem("w_act")
        w_hi = sem("w_hi")
        w_lo = sem("w_lo")
        w_pe = sem("w_pe")
        x_in = sem("x_in")
        x_res = sem("x_res")
        qk_out = sem("qk_out")
        qk_in = sem("qk_in")
        m_out = sem("m_out")
        m_in = sem("m_in")
        y_out = sem("y_out")
        pe_proj = sem("pe_proj")
        pe_max = sem("pe_max")
        pe_mrow = sem("pe_mrow")
        pe_unit = sem("pe_unit")
        pe_av = sem("pe_av")
        pe_o = sem("pe_o")
        pe_tail = sem("pe_tail")
        pe_up = sem("pe_up")
        act_xT = sem("act_xT")
        act_exp = sem("act_exp")
        act_uT = sem("act_uT")
        act_zT = sem("act_zT")
        act_x1T = sem("act_x1T")
        act_gate = sem("act_gate")
        act_silu = sem("act_silu")
        pool_mask = sem("pool_mask")
        dve_part = sem("dve_part")
        dve_qk = sem("dve_qk")
        dve_max = sem("dve_max")
        dve_mrow = sem("dve_mrow")
        dve_o = sem("dve_o")
        dve_z = sem("dve_z")
        dve_wo = sem("dve_wo")
        dve_x1 = sem("dve_x1")
        dve_x1lo = sem("dve_x1lo")
        dve_lg = sem("dve_lg")
        dve_cw = sem("dve_cw")
        dve_hid = sem("dve_hid")
        ch0 = sem("ch0")
        pe_down = sem("pe_down")
        pe_x2 = sem("pe_x2")
        pe_s1 = sem("pe_s1")
        pe_pT = sem("pe_pT")
        pe_av1 = sem("pe_av1")
        pe_x3 = sem("pe_x3")
        pe_h1 = sem("pe_h1")
        pe_y = sem("pe_y")
        act_x2T = sem("act_x2T")
        act_qkv = sem("act_qkv")
        act_p1 = sem("act_p1")
        act_x3 = sem("act_x3")
        act_h1 = sem("act_h1")
        act_sin = sem("act_sin")
        pool_x3 = sem("pool_x3")
        dve_y2 = sem("dve_y2")
        dve_x2 = sem("dve_x2")
        dve_q1 = sem("dve_q1")
        dve_k1 = sem("dve_k1")
        dve_m1 = sem("dve_m1")
        dve_pT = sem("dve_pT")
        dve_r3 = sem("dve_r3")
        dve_x3 = sem("dve_x3")
        dve_x3lo = sem("dve_x3lo")
        dve_ang = sem("dve_ang")
        dve_act = sem("dve_act")
        dve_y = sem("dve_y")
        ch1 = sem("ch1")
        NG = len(MAX_GROUPS)
        NQ = G * NU

        block = ctx.enter_context(nc.Block())

        x_v = x.rearrange("b (t p) d -> b p t d", p=P)
        out_v = out.rearrange("b (t p) d -> b p t d", p=P)

        def row(ap, n):
            return ap.rearrange("(a n) -> a n", a=1).to_broadcast([P, n])


        N_SMALL = 23
        Z_DOWN, Z_CONST = 2, 8

        def first(b):
            return isinstance(b, int) and b == 0

        @block.sync
        def _(sp):
            loads = []

            def load(dst, src):
                loads.append(sp.dma_start(dst, src).then_inc(w_in, 16))

            def load_x(b):
                if not first(b):
                    sp.wait_ge(pe_proj, 4 * (b - 1) + 1)
                    sp.wait_ge(x_res, 1 * b)
                sp.dma_start(xin[:], x_v[bass.ds(b, 1)].rearrange("a p t d -> p (a t) d")).then_inc(x_in, 16)

            def restack(b):
                sp.wait_ge(dve_qk, 2 * b + 1)
                sp.dma_start(q_scr.rearrange("a p n -> p a n"), qparts[:]).then_inc(qk_out, 16)
                sp.wait_ge(dve_qk, 2 * b + 2)
                sp.dma_start(k_scr.rearrange("a p n -> p a n"), kparts[:]).then_inc(qk_out, 16)
                sp.wait_ge(qk_out, 32 * b + 32)
                for t in range(TERMS):
                    for dst, src, part in ((kstack, k_scr, t % PARTS), (qstack, q_scr, t // PARTS)):
                        sp.dma_start(dst[HD * t:HD * (t + 1)],
                                     src[part].rearrange("(h d) n -> d h n", d=HD)).then_inc(qk_in, 16)

            def restack_max(b):
                sp.wait_ge(dve_mrow, 2 * b + 2)
                sp.dma_start(m_scr.rearrange("a h n -> h a n"), mparts[:]).then_inc(m_out, 16)
                sp.wait_ge(m_out, 16 * b + 16)
                sp.dma_start(qstack[ROWS:ROWS + PARTS], m_scr).then_inc(m_in, 16)

            def store(b):
                sp.wait_ge(dve_y, 1 * b + 1)
                sp.dma_start(out_v[bass.ds(b, 1)].rearrange("a p t d -> p (a t) d"), y[:]).then_inc(y_out, 16)

            load_x(0)
            sp.wait_ge(w_pool, 1)
            for n, v in enumerate((theta, w_real, w_imag, fb1)):
                load(vec_rows[NF * n:NF * (n + 1), :], v.rearrange("(f p) -> f p", p=P))
            load(vec_rows[4 * NF:4 * NF + E, :], gate_w[0:E, :])
            for n, v in enumerate((bq0, ln_g, ln_b, bk0)):
                k = 4 * NF + E + n
                load(vec_rows[k:k + 1, 0:v.shape[0]], v.rearrange("(a n) -> a n", a=1))
            load(wq0[:], Wq0)
            load(wk0[:], Wk0)
            load(wv0[:], Wv0)
            load(bv_r[:], row(bv0, KV))
            load(bo_r[:], row(bo0, D))
            load(wo0[:], Wo0)
            load(f1[:], fW1)
            load(b2_r[:], row(fb2, D))
            load(wv1[:], Wv1)
            for half in range(2):
                load(wq1[:, half, :], Wq1)
                load(wk1[:, half, :], Wk1)
            load(f2[:], fW2.rearrange("(f p) d -> p f d", p=P))
            assert len(loads) == N_SMALL, len(loads)
            sp.dma_start(stage[:, 0], w1[0:E].rearrange("e d n -> d e n")).then_inc(w_up_in, 16)
            sp.dma_start(stage[:, 1], w3[0:E].rearrange("e d n -> d e n")).then_inc(w_up_in, 16)
            sp.wait_ge(w_zero, 2)
            restack(0)
            sp.wait_ge(w_pool, Z_DOWN)
            for e in range(E):
                n0 = e * (FULL + 1)
                sp.dma_start(down[:, n0:n0 + FULL, :],
                             w2[e, 0:FULL * P, :].rearrange("(j p) d -> p j d", p=P)).then_inc(w_down_in, 16)
                p0 = TAIL * (e % 2)
                sp.dma_start(down[p0:p0 + TAIL, n0 + FULL, :], w2[e, FULL * P:, :]).then_inc(w_down_in, 16)
            restack_max(0)
            with sp.Fori(1, B) as b:
                load_x(b)
                restack(b)
                restack_max(b)
                store(b - 1)
            store(B - 1)
            sp.wait_ge(y_out, 16 * B + 1)

        @block.gpsimd
        def _(pool):
            gp = nc.gpsimd
            gp.memset(vec_rows[:], 0.0).then_inc(w_pool, 1)
            gp.memset(down[:, FULL::FULL + 1, :], 0.0).then_inc(w_pool, 1)
            pool.wait_ge(w_pool, 1)
            gp.memset(ident[:], 0.0)
            gp.memset(future_h[:], 0.0)
            gp.memset(before[:], 1.0)
            gp.memset(carry[:], 0.0)
            gp.memset(vext[:], 0.0).then_inc(w_pool, 1)
            pool.wait_ge(w_pool, 3)
            gp.affine_select(out=ident[:], in_=ident[:], compare_op=ALU.not_equal, fill=1.0, base=0,
                             pattern=[[-1, P]], channel_multiplier=1).then_inc(w_pool, 1)
            gp.affine_select(out=future_h[:], in_=future_h[:], compare_op=ALU.is_ge, fill=NEG, base=0,
                             pattern=[[0, 4], [-1, P]], channel_multiplier=1).then_inc(w_pool, 1)
            gp.affine_select(out=before[:], in_=before[:], compare_op=ALU.is_gt, fill=0.0, base=0,
                             pattern=[[1, E], [-1, E]], channel_multiplier=0).then_inc(w_pool, 1)
            gp.memset(vext[:, :, :, HD:HD + 1], 1.0).then_inc(w_pool, 1)
            pool.wait_ge(w_pool, 4)
            gp.tensor_copy(ident_h[:], ident[:]).then_inc(w_pool, 1)
            gp.memset(y[:, 0, 0:1], 0.0).then_inc(y_out, 1)

            def residual_x(b):
                pool.wait_ge(x_in, 16 * b + 16)
                if not first(b):
                    pool.wait_ge(dve_wo, 1 * b)
                gp.tensor_tensor(xres[:], xin[:], bo_r[:].unsqueeze(1).to_broadcast([P, NT, D]),
                                 ALU.add).then_inc(x_res, 1)

            def masks(b):
                for g in range(G):
                    for u in range(NU):
                        n = NU * g + u
                        pool.wait_ge(act_exp, NQ * b + n + 1)
                        gp.tensor_tensor(carry[:, n + 1:n + 2], carry[:, 0:1], carry[:, 0:1], ALU.add)
                        pr = probs[:, g % 2, u, :]
                        if u < H:
                            spots = [(pr[:, 0:P], [[1, P]]),
                                     (pr[:, 512:512 + 2 * P].rearrange("p (a q) -> p a q", a=2), [[0, 2], [1, P]])]
                        else:
                            spots = [(pr.rearrange("p (a q) -> p a q", a=H)[:, :, 0:P], [[0, H], [1, P]])]
                        for spot, pattern in spots:
                            last = gp.affine_select(out=spot, in_=spot, compare_op=ALU.is_ge, fill=0.0, base=0,
                                                    pattern=pattern, channel_multiplier=-1)
                        last.then_inc(pool_mask, 1)

            def residual_x3(b):
                pool.wait_ge(pe_x3, 1 * b + 1)
                gp.tensor_tensor(x3[:], x3[:], b2_r[:].unsqueeze(1).to_broadcast([P, NT, D]),
                                 ALU.add).then_inc(pool_x3, 1)

            pool.wait_ge(w_in, 16 * N_SMALL)
            residual_x(0)
            for n, (hi, lo) in enumerate(zip(up_hi, up_lo)):
                for k, (dst, src) in enumerate(tiles_of(lo, stage[:, n])):
                    pool.wait_ge(w_hi, 3 * n + k + 1)
                    gp.tensor_tensor(dst, src, tiles_of(hi, stage[:, n])[k][0].bitcast(FP32),
                                     ALU.subtract).then_inc(w_lo, 1)
            pool.wait_ge(w_hi, 7)
            gp.tensor_tensor(f1_lo[:], f1[:], f1_hi[:].bitcast(FP32), ALU.subtract).then_inc(w_lo, 1)
            masks(0)
            with pool.Fori(1, B) as b:
                residual_x(b)
                masks(b)
                residual_x3(b - 1)
            residual_x3(B - 1)

        @block.scalar
        def _(act):
            sc = nc.scalar

            def xT_out(b):
                act.wait_ge(pe_proj, 4 * b + 1)
                if not first(b):
                    act.wait_ge(pe_proj, 4 * b)
                sc.activation(xT[:], ps[:, 4, :], ACT.Copy).then_inc(act_xT, 1)

            def exps(b, n):
                g, u = n // NU, n % NU
                act.wait_ge(pe_unit, NQ * b + n + 1)
                if n == 0 and first(b):
                    act.wait_ge(w_lo, 7)
                if g < 2:
                    if u == 0 and not first(b):
                        act.wait_ge(pe_down, NT * b)
                else:
                    act.wait_ge(pe_av, G * b + g - 1)
                pair = 2 * (n % 2)
                sc.activation(probs[:, g % 2, u, :].rearrange("p (a n) -> p a n", a=2),
                              ps[:, pair:pair + 2, :], ACT.Exp, scale=SCALE0).then_inc(act_exp, 1)

            def uT_out(b, g):
                act.wait_ge(pe_av, G * b + g + 1)
                if g == 0 and not first(b):
                    act.wait_ge(pe_o, NT * b)
                sc.activation(uT[:, g, :], ps[:, (7, 4)[g % 2], :], ACT.Copy).then_inc(act_uT, 1)

            def zT_out(b):
                act.wait_ge(pe_tail, 4 * b + 1)
                sc.activation(zT[:], ps[:, 7, :], ACT.Identity, bias=lnb_c,
                              scale=lng_c).then_inc(act_zT, 1)

            def x1T_out(b):
                act.wait_ge(pe_tail, 4 * b + 3)
                if not first(b):
                    act.wait_ge(pe_up, 2 * NM * b)
                    act.wait_ge(dve_x1lo, 1 * b)
                sc.activation(x1T[:], ps[:, 7, :], ACT.Copy).then_inc(act_x1T, 1)
                sc.activation(x1_hi[:], ps[:, 7, :], ACT.Copy).then_inc(act_x1T, 1)

            def gate_exp(b):
                act.wait_ge(dve_lg, 2 * b + 2)
                sc.activation(lgx[:, 1], lgx[:, 0], ACT.Exp).then_inc(act_gate, 1)

            def silus(b, m):
                act.wait_ge(pe_up, 2 * NM * b + 2 * m + 1)
                if not (first(b) and m < 2):
                    act.wait_ge(dve_hid, NM * b + m - 1)
                sc.activation(silu[:, m % 2, :], ps[:, 2 * (m % 2), :], ACT.Silu).then_inc(act_silu, 1)

            def x2T_out(b):
                act.wait_ge(pe_x2, 4 * b + 1)
                sc.activation(x2T[:], ps[:, 5, :], ACT.Copy).then_inc(act_x2T, 1)

            def qkv1_out(b):
                act.wait_ge(pe_x2, 4 * b + 2)
                sc.activation(q1[:], ps[:, 6, :], ACT.Copy).then_inc(act_qkv, 1)
                act.wait_ge(pe_x2, 4 * b + 3)
                sc.activation(k1a[:], ps[:, 5, :], ACT.Copy).then_inc(act_qkv, 1)

            def v1_out(b):
                act.wait_ge(pe_x2, 4 * b + 4)
                sc.activation(two_a[:, 1, :], ps[:, 6, :], ACT.Copy).then_inc(act_qkv, 1)

            def exp1(b, qt):
                act.wait_ge(dve_m1, NT * b + qt + 1)
                if qt:
                    act.wait_ge(pe_pT, NT * b + qt)
                n = (qt + 1) * P
                sc.activation(prob1[:, 0:n], ps[:, 5, 0:n], ACT.Exp, bias=nmax1[:, 1, qt:qt + 1], scale=SCALE1,
                              accum_out=den1[:, 0, qt:qt + 1]).then_inc(act_p1, 1)

            def x3_out(b):
                act.wait_ge(pe_x3, 1 * b + 1)
                sc.activation(x3_hi[:], ps[:, 6, :], ACT.Copy).then_inc(act_x3, 1)

            def hidden1_out(b, f):
                act.wait_ge(pe_h1, NF * b + f + 1)
                if f >= 2:
                    act.wait_ge(dve_act, NF * b + f - 1)
                sc.activation(hid1[:, f % 2, :], ps[:, 5 + f % 2, :], ACT.Identity,
                              bias=fb1_c[:, f:f + 1]).then_inc(act_h1, 1)

            def sines(b, f):
                act.wait_ge(dve_ang, NF * b + f + 1)
                sc.activation(ang[:, f % 2, :], ang[:, f % 2, :], ACT.Sin, scale=TURN).then_inc(act_sin, 1)

            xT_out(0)
            act.wait_ge(w_up_in, 32)
            for n, hi in enumerate(up_hi):
                for dst, src in tiles_of(hi, stage[:, n]):
                    sc.activation(dst, src, ACT.Copy).then_inc(w_hi, 1)
            sc.activation(f1_hi[:], f1[:], ACT.Copy).then_inc(w_hi, 1)
            act.wait_ge(w_dve, W_TURNS)
            sc.activation(th[:, 4:6, :], th[:, 2:4, :], ACT.Sin, scale=TURN).then_inc(w_act, 1)

            def attention(b, back):
                for n in range(NQ):
                    exps(b, n)
                    if n % NU == 2 and n > NU:
                        uT_out(b, n // NU - 1)
                    for step in back.get(n, ()):
                        step()
                uT_out(b, G - 1)

            def middle(b):
                zT_out(b)
                x1T_out(b)
                gate_exp(b)

            attention(0, {})
            middle(0)
            for m in range(NM):
                silus(0, m)
            with act.Fori(1, B) as b:
                xT_out(b)
                x2T_out(b - 1)
                qkv1_out(b - 1)
                v1_out(b - 1)
                for n in range(NQ):
                    exps(b, n)
                    if n % NU == 2 and n > NU:
                        uT_out(b, n // NU - 1)
                    if n % NU == 4:
                        exp1(b - 1, n // NU)
                uT_out(b, G - 1)
                zT_out(b)
                x3_out(b - 1)
                x1T_out(b)
                gate_exp(b)
                for m in range(NM):
                    silus(b, m)
                    if m % 5 == 1 and m // 5 < NF:
                        hidden1_out(b - 1, m // 5)
                    if m % 5 == 3 and m // 5 < NF:
                        sines(b - 1, m // 5)
            last = B - 1
            x2T_out(last)
            qkv1_out(last)
            v1_out(last)
            for qt in range(NT):
                exp1(last, qt)
            x3_out(last)
            for f in range(NF):
                hidden1_out(last, f)
                if f:
                    sines(last, f - 1)
            sines(last, NF - 1)

        @block.tensor
        def _(pe):
            last_b = B - 1
            mm, tr = nc.tensor.matmul, nc.tensor.transpose

            def split3(dst, hi, lo, vhi, vlo):
                mm(dst, hi, vhi, start=True, stop=False)
                mm(dst, hi, vlo, start=False, stop=False)
                return mm(dst, lo, vhi, start=False, stop=True)

            def cols(t):
                return slice(t * P, (t + 1) * P)

            def project(b):
                pe.wait_ge(x_in, 16 * b + 16)
                if not first(b):
                    pe.wait_ge(dve_lg, 2 * b)
                for t in range(NT):
                    last = tr(ps[:, 4, cols(t)], xin[:, t, :], ident[:])
                last.then_inc(pe_proj, 1)
                pe.wait_ge(act_xT, 1 * b + 1)
                mm(ps[:, 7, :], wq0[:], xT[:], start=True, stop=True).then_inc(pe_proj, 1)
                mm(ps[0:KV, 4, :], wk0[:], xT[:], start=True, stop=True).then_inc(pe_proj, 1)
                pe.wait_ge(dve_part, 3 * b + 1)
                for t in range(NT):
                    last = mm(ps[:, 7, KV * t:KV * (t + 1)], xT[:, cols(t)], wv0[:], start=True, stop=True)
                last.then_inc(pe_proj, 1)

            def scores_for_max(b, j):
                qt, h0, hn = MAX_GROUPS[j]
                n, bank = (qt + 1) * P, (4, 7)[j % 2]
                if j == 0:
                    pe.wait_ge(qk_in, 32 * TERMS * (b + 1))
                    pe.wait_ge(dve_part, 3 * b + 2)
                elif j == 1:
                    pe.wait_ge(dve_part, 3 * b + 3)
                else:
                    pe.wait_ge(dve_max, NG * b + j - 1)
                for k in range(hn):
                    dst = ps[:, bank, k * n:(k + 1) * n]
                    mm(dst, qstack[0:ROWS, h0 + k, cols(qt)], kstack[0:ROWS, (h0 + k) % H, 0:n],
                       start=True, stop=False)
                    last = mm(dst[:, qt * P:n], ident_h[:], future_h[:, 0, :], start=False, stop=True)
                last.then_inc(pe_max, 1)

            def transpose_max(b):
                pe.wait_ge(dve_max, NG * (b + 1))
                for t in range(NT):
                    last = tr(ps[0:NH, 4, cols(t)], negmax[:, t, :], ident[:])
                last.then_inc(pe_mrow, 1)

            def exact_unit(b, n):
                g, u = n // NU, n % NU
                pair = 2 * (n % 2)
                if n == 0:
                    pe.wait_ge(m_in, 16 * b + 16)
                if n < 2:
                    if not first(b):
                        pe.wait_ge(dve_hid, NM * b)
                else:
                    pe.wait_ge(act_exp, NQ * b + n - 1)
                for kb, h, col, q0 in UNITS[u]:
                    n_q = S - q0
                    last = mm(ps[:, pair + col // 512, col % 512:col % 512 + n_q], kstack[:, h, cols(kb)],
                              qstack[:, H * g + h, q0:S], start=True, stop=True)
                last.then_inc(pe_unit, 1)

            def values(b, g):
                bank = (7, 4)[g % 2]
                pe.wait_ge(pool_mask, NQ * b + NU * (g + 1))
                if g == 0:
                    pe.wait_ge(dve_part, 3 * b + 3)
                elif g == 1:
                    pe.wait_ge(dve_mrow, 2 * b + 1)
                else:
                    pe.wait_ge(act_uT, G * b + g - 1)
                for kb in range(NT):
                    for h in range(H):
                        u, col, q0 = PLACE[kb, h]
                        last = mm(ps[32 * h:32 * h + 32, bank, q0:S], vext[:, kb, h, :],
                                  probs[:, g % 2, u, col:col + S - q0], start=(kb == 0), stop=(kb == NT - 1))
                last.then_inc(pe_av, 1)

            def transpose_o(b, t):
                if t == 0:
                    pe.wait_ge(act_uT, G * (b + 1))
                if t >= 2:
                    pe.wait_ge(dve_o, NT * b + t - 1)
                for g in range(G):
                    last = tr(ps[:, (7, 4)[t % 2], cols(g)], uT[:, g, cols(t)], ident[:])
                last.then_inc(pe_o, 1)

            def transpose_z(b):
                pe.wait_ge(dve_z, 1 * b + 1)
                for t in range(NT):
                    last = tr(ps[:, 7, cols(t)], attn[:, t, :], ident[:])
                last.then_inc(pe_tail, 1)

            def project_out(b):
                pe.wait_ge(act_zT, 1 * b + 1)
                for t in range(NT):
                    last = mm(ps[:, 4, cols(t)], zT[:, cols(t)], wo0[:], start=True, stop=True)
                last.then_inc(pe_tail, 1)

            def transpose_x1(b):
                pe.wait_ge(dve_x1, 1 * b + 1)
                for t in range(NT):
                    last = tr(ps[:, 7, cols(t)], x1[:, t, :], ident[:])
                last.then_inc(pe_tail, 1)

            def gate(b):
                pe.wait_ge(act_x1T, 2 * b + 1)
                for t in range(NT):
                    last = mm(ps[:, 4, E * t:E * (t + 1)], x1T[:, cols(t)], gateT, start=True, stop=True)
                last.then_inc(pe_tail, 1)

            def experts_up(b, m):
                pair = 2 * (m % 2)
                if m == 0:
                    pe.wait_ge(dve_x1lo, 1 * b + 1)
                    pe.wait_ge(act_exp, NQ * (b + 1))
                if m >= 2:
                    pe.wait_ge(dve_hid, NM * b + m - 1)
                for n in range(2):
                    split3(ps[:, pair + n, :], up_hi[n][:, m, :], up_lo[n][:, m, :],
                           x1_hi[:], x1_lo[:]).then_inc(pe_up, 1)

            def experts_down(b, t):
                if t == 0:
                    pe.wait_ge(dve_hid, NM * (b + 1))
                    if b is last_b:
                        pe.wait_ge(dve_y, b)
                if t >= 2:
                    pe.wait_ge(dve_y2, NT * b + t - 1)
                for e in range(E):
                    for j, tile in enumerate(EXPERT_TILES[e]):
                        last = mm(ps[:, 5 + t % 2, cols(e)], hidT[:, tile, cols(t)],
                                  down[:, e * (FULL + 1) + j, :], start=(e == 0 and j == 0),
                                  stop=(j == FULL), skip_group_check=True)
                last.then_inc(pe_down, 1)

            def project1(b):
                pe.wait_ge(dve_x2, 1 * b + 1)
                for t in range(NT):
                    last = tr(ps[:, 5, cols(t)], x2[:, t, :], ident[:])
                last.then_inc(pe_x2, 1)
                pe.wait_ge(act_x2T, 1 * b + 1)
                mm(ps[:, 6, :], wq1[:].rearrange("p a d -> p (a d)"), x2T[:], start=True, stop=True).then_inc(pe_x2, 1)
                mm(ps[:, 5, :], wk1[:].rearrange("p a d -> p (a d)"), x2T[:], start=True, stop=True).then_inc(pe_x2, 1)

            def project1_v(b):
                pe.wait_ge(dve_q1, 1 * b + 1)
                for t in range(NT):
                    last = mm(ps[:, 6, cols(t)], x2T[:, cols(t)], wv1[:], start=True, stop=True)
                last.then_inc(pe_x2, 1)

            def scores1(b, t):
                if t == 0:
                    pe.wait_ge(dve_k1, 1 * b + 1)
                else:
                    pe.wait_ge(dve_r3, NT * b + t)
                n = (t + 1) * P
                mm(ps[:, 5, 0:n], q1[:, cols(t)], k1a[:, 0:n], start=True, stop=False)
                mm(ps[:, 5, 0:n], q1[:, cols(t)], k1b[:, 0:n], start=False, stop=False)
                mm(ps[:, 5, t * P:n], ident_h[:], future_h[:, 0, :], start=False, stop=True).then_inc(pe_s1, 1)

            def transpose_p1(b, t):
                pe.wait_ge(act_p1, NT * b + t + 1)
                if t == 0:
                    pe.wait_ge(act_qkv, 3 * b + 3)
                else:
                    pe.wait_ge(dve_pT, NT * b + t)
                for kb in range(t + 1):
                    last = tr(ps[:, 6, cols(kb)], prob1[:, cols(kb)], ident[:])
                last.then_inc(pe_pT, 1)

            def values1(b, t):
                pe.wait_ge(dve_pT, NT * b + t + 1)
                for kb in range(t + 1):
                    last = mm(ps[:, 5, 0:D], probT1[:, cols(kb)], v1[:, kb, :], start=(kb == 0), stop=(kb == t))
                last.then_inc(pe_av1, 1)

            def transpose_x3(b):
                pe.wait_ge(dve_x3, 1 * b + 1)
                for t in range(NT):
                    last = tr(ps[:, 6, cols(t)], x3[:, t, :], ident[:])
                last.then_inc(pe_x3, 1)

            def hidden1(b, f):
                if f == 0:
                    pe.wait_ge(dve_x3lo, 1 * b + 1)
                if f >= 2:
                    pe.wait_ge(act_h1, NF * b + f - 1)
                split3(ps[:, 5 + f % 2, :], f1_hi[:, cols(f)], f1_lo[:, cols(f)],
                       x3_hi[:], x3_lo[:]).then_inc(pe_h1, 1)

            def output1(b):
                pe.wait_ge(act_h1, NF * (b + 1))
                pe.wait_ge(dve_act, NF * (b + 1))
                for t in range(NT):
                    for f in range(NF):
                        last = mm(ps[:, 5, cols(t)], actT[:, f, cols(t)], f2[:, f, :], start=(f == 0),
                                  stop=(f == NF - 1))
                last.then_inc(pe_y, 1)

            pe.wait_ge(w_pool, Z_CONST)
            pe.wait_ge(w_in, 16 * N_SMALL)
            tr(ps[:, 5, 0:N_VEC], vec_rows[:], ident[0:N_VEC, 0:N_VEC]).then_inc(w_pe, 1)
            project(0)
            for j in range(NG):
                scores_for_max(0, j)
            transpose_max(0)
            for n in range(NQ):
                exact_unit(0, n)
                if n % NU == 2 and n > NU:
                    values(0, n // NU - 1)
            values(0, G - 1)
            for t in range(NT):
                transpose_o(0, t)
            transpose_z(0)
            project_out(0)
            transpose_x1(0)
            pe.wait_ge(w_dve, 1)
            gate(0)
            pe.wait_ge(w_lo, 7)
            for m in range(NM):
                experts_up(0, m)
            pe.wait_ge(w_down_in, 16 * 2 * E)
            with pe.Fori(1, B) as b:
                project(b)
                for j in range(NG):
                    scores_for_max(b, j)
                    if j % 11 == 10:
                        experts_down(b - 1, j // 11)
                transpose_max(b)
                project1(b - 1)
                project1_v(b - 1)
                for n in range(NQ):
                    exact_unit(b, n)
                    if n % NU == 2 and n > NU:
                        values(b, n // NU - 1)
                    if n % NU == 1:
                        scores1(b - 1, n // NU)
                    if n % NU == 4:
                        transpose_p1(b - 1, n // NU)
                    if n % NU == 0 and n:
                        values1(b - 1, n // NU - 1)
                values(b, G - 1)
                values1(b - 1, NT - 1)
                for t in range(NT):
                    transpose_o(b, t)
                transpose_z(b)
                transpose_x3(b - 1)
                project_out(b)
                transpose_x1(b)
                gate(b)
                for m in range(NM):
                    experts_up(b, m)
                    if m % 5 == 0 and m // 5 < NF:
                        hidden1(b - 1, m // 5)
                output1(b - 1)
            last_b = B - 1
            for t in range(NT):
                experts_down(last_b, t)
            project1(last_b)
            project1_v(last_b)
            for t in range(NT):
                scores1(last_b, t)
                transpose_p1(last_b, t)
                values1(last_b, t)
            transpose_x3(last_b)
            for f in range(NF):
                hidden1(last_b, f)
            output1(last_b)

        @block.vector
        def _(dve):
            ve = nc.vector
            front = Chain(dve, ch0, N_FRONT)
            back = Chain(dve, ch1, N_BACK)

            def per_tile(ap):
                return ap.unsqueeze(2).to_broadcast([P, NT, D])

            def layer_norm(chain, n, src, dst, done):
                link, s = chain.link, ln_s[n]
                for t in range(NT):
                    last = ve.bn_stats(stats[n][:, t, :], src[:, t, :])
                link(last)
                ve.memset(s[:, 2, 0:1], 0.0)
                for t in range(NT):
                    last = ve.bn_aggr(mv[n][:, t, :], stats[n][:, t, :])
                link(last)
                link(ve.tensor_scalar(s[:, 0, :], mv[n][:, :, 1], EPS, None, ALU.add))
                link(ve.tensor_scalar(s[:, 1, :].bitcast(I32), s[:, 0, :].bitcast(I32), -0.5, RSQRT_SEED,
                                      ALU.mult, ALU.add))
                for _ in range(3):
                    link(ve.tensor_tensor(s[:, 2, :], s[:, 1, :], s[:, 1, :], ALU.mult))
                    link(ve.scalar_tensor_tensor(s[:, 3, :], s[:, 2, :], -0.5, s[:, 0, :], ALU.mult, ALU.mult))
                    link(ve.scalar_tensor_tensor(s[:, 1, :], s[:, 3, :], 1.5, s[:, 1, :], ALU.add, ALU.mult))
                for t in range(NT):
                    last = ve.tensor_scalar(dst[:, t, :], src[:, t, :], mv[n][:, t, 0:1], s[:, 1, t:t + 1],
                                            ALU.subtract, ALU.mult)
                last.then_inc(done, 1)

            def in_parts(chain, dst, src, bias, rows, read):
                work = part_f[0:rows, :]
                ve.tensor_scalar(work, src, bias, None, ALU.add).then_inc(dve_part, 1)
                dve.wait_ge(dve_part, read)
                for a in range(PARTS):
                    ins = ve.tensor_copy(dst[:, a, :], work)
                    if a < PARTS - 1:
                        chain.link(ins)
                        chain.link(ve.tensor_tensor(work, work, dst[:, a, :], ALU.subtract))
                return ins

            def parts(b):
                front.begin(b)
                dve.wait_ge(pe_proj, 4 * b + 2)
                if not first(b):
                    dve.wait_ge(qk_out, 32 * b)
                in_parts(front, qparts, ps[:, 7, :], bq_c, P, 3 * b + 1).then_inc(dve_qk, 1)
                dve.wait_ge(dve_qk, 2 * b + 1)
                dve.wait_ge(pe_proj, 4 * b + 3)
                in_parts(front, kparts, ps[0:KV, 4, :], bk_c[0:KV], KV, 3 * b + 2).then_inc(dve_qk, 1)
                dve.wait_ge(pe_proj, 4 * b + 4)
                if not first(b):
                    dve.wait_ge(pe_av, G * b)
                ve.tensor_tensor(vext[:, :, :, 0:HD],
                                 ps[:, 7, 0:NT * KV].rearrange("p (t h d) -> p t h d", t=NT, h=H),
                                 bv_r[:].rearrange("p (a h d) -> p a h d", a=1, h=H).to_broadcast([P, NT, H, HD]),
                                 ALU.add).then_inc(dve_part, 1)

            def maxima(b, j):
                qt, h0, hn = MAX_GROUPS[j]
                n = (qt + 1) * P
                dve.wait_ge(pe_max, NG * b + j + 1)
                if j == 0 and not first(b):
                    dve.wait_ge(pe_mrow, 1 * b)
                ve.tensor_reduce(negmax[:, qt, h0:h0 + hn],
                                 ps[:, (4, 7)[j % 2], 0:hn * n].rearrange("p (h n) -> p h n", h=hn),
                                 axis=AX.X, op=ALU.max, negate=True).then_inc(dve_max, 1)

            def max_parts(b):
                dve.wait_ge(pe_mrow, 1 * b + 1)
                if not first(b):
                    dve.wait_ge(m_out, 16 * b)
                ve.tensor_copy(mrow[:], ps[0:NH, 4, :]).then_inc(dve_mrow, 1)
                dve.wait_ge(dve_mrow, 2 * b + 1)
                for a in range(PARTS):
                    ins = ve.tensor_copy(mparts[:, a, :], mrow[:])
                    if a < PARTS - 1:
                        front.link(ins)
                        front.link(ve.tensor_tensor(mrow[:], mrow[:], mparts[:, a, :], ALU.subtract))
                ins.then_inc(dve_mrow, 1)

            def divide(b, t):
                dve.wait_ge(pe_o, NT * b + t + 1)
                if t == 0 and not first(b):
                    dve.wait_ge(dve_z, 1 * b)
                heads = ps[:, (7, 4)[t % 2], :].rearrange("p (h c) -> p h c", c=32)
                front.link(ve.reciprocal(rden0[:, t, :], heads[:, :, HD]))
                ve.tensor_tensor(att[:, t, :].rearrange("p (h c) -> p h c", c=HD), heads[:, :, 0:HD],
                                 rden0[:, t, :].unsqueeze(2).to_broadcast([P, NH, HD]),
                                 ALU.mult).then_inc(dve_o, 1)

            def norm_z(b):
                dve.wait_ge(dve_o, NT * (b + 1))
                if not first(b):
                    dve.wait_ge(pe_tail, 4 * b)
                layer_norm(front, 0, att, attn, dve_z)

            def norm_x1(b):
                dve.wait_ge(pe_tail, 4 * b + 2)
                dve.wait_ge(x_res, 1 * b + 1)
                ve.tensor_tensor(res1[:].rearrange("p t d -> p (t d)"), ps[:, 4, :],
                                 xres[:].rearrange("p t d -> p (t d)"), ALU.add).then_inc(dve_wo, 1)
                dve.wait_ge(dve_wo, 1 * b + 1)
                if not first(b):
                    dve.wait_ge(dve_y2, NT * b)
                layer_norm(front, 0, res1, x1, dve_x1)

            def x1_lower(b):
                dve.wait_ge(act_x1T, 2 * b + 2)
                if not first(b):
                    dve.wait_ge(pe_up, 2 * NM * b)
                ve.tensor_tensor(x1_lo[:], x1T[:], x1_hi[:].bitcast(FP32), ALU.subtract).then_inc(dve_x1lo, 1)

            def gate_logits(b):
                dve.wait_ge(pe_tail, 4 * b + 4)
                ve.tensor_copy(lg[:].rearrange("p t e -> p (t e)"), ps[:, 4, 0:NT * E]).then_inc(dve_lg, 1)
                dve.wait_ge(dve_lg, 2 * b + 1)
                front.link(ve.tensor_reduce(lgs[:, 0, :], lg[:], axis=AX.X, op=ALU.max))
                if not first(b):
                    dve.wait_ge(act_gate, 1 * b)
                ve.tensor_tensor(lgx[:, 0], lg[:], lgs[:, 0, :].unsqueeze(2).to_broadcast([P, NT, E]),
                                 ALU.subtract).then_inc(dve_lg, 1)

            def gate_weights(b):
                other = lg[:].unsqueeze(2).to_broadcast([P, NT, E, E])
                own = lg[:].unsqueeze(3).to_broadcast([P, NT, E, E])
                ve.tensor_tensor(cmp4[:, 0], other, own, ALU.is_gt)
                front.link(ve.tensor_tensor(cmp4[:, 1], other, own, ALU.is_equal))
                front.link(ve.tensor_tensor(cmp4[:, 1].rearrange("p t e j -> p t (e j)"),
                                            cmp4[:, 1].rearrange("p t e j -> p t (e j)"),
                                            before[:].rearrange("p e j -> p (e j)").unsqueeze(1)
                                            .to_broadcast([P, NT, E * E]), ALU.mult))
                front.link(ve.tensor_tensor(cmp4[:, 0], cmp4[:, 0], cmp4[:, 1], ALU.add))
                front.link(ve.tensor_reduce(lgx[:, 2], cmp4[:, 0], axis=AX.X, op=ALU.add))
                front.link(ve.tensor_scalar(lgx[:, 2], lgx[:, 2], 2.0, None, ALU.is_lt))
                dve.wait_ge(act_gate, 1 * b + 1)
                front.link(ve.tensor_tensor(lgx[:, 2], lgx[:, 2], lgx[:, 1], ALU.mult))
                front.link(ve.tensor_reduce(lgs[:, 1, :], lgx[:, 2], axis=AX.X, op=ALU.add))
                front.link(ve.reciprocal(lgs[:, 2, :], lgs[:, 1, :]))
                ve.tensor_tensor(cw[:], lgx[:, 2], lgs[:, 2, :].unsqueeze(2).to_broadcast([P, NT, E]),
                                 ALU.mult).then_inc(dve_cw, 1)
                front.end()

            def expert_hidden(b, m):
                dve.wait_ge(act_silu, NM * b + m + 1)
                dve.wait_ge(pe_up, 2 * NM * b + 2 * m + 2)
                if m == 0:
                    dve.wait_ge(pe_av, G * (b + 1))
                ve.tensor_tensor(hidT[:, m, :], silu[:, m % 2, :], ps[:, 2 * (m % 2) + 1, :],
                                 ALU.mult).then_inc(dve_hid, 1)

            def mix(b, t):
                if t == 0:
                    back.begin(b)
                    dve.wait_ge(dve_cw, 1 * b + 1)
                dve.wait_ge(pe_down, NT * b + t + 1)
                src = x1
                for e in range(E):
                    ins = ve.scalar_tensor_tensor(res[:, t, :], ps[:, 5 + t % 2, e * D:(e + 1) * D],
                                                  cw[:, t, e:e + 1], src[:, t, :], ALU.mult, ALU.add)
                    src = res
                    if e < E - 1:
                        back.link(ins)
                ins.then_inc(dve_y2, 1)

            def norm_x2(b):
                dve.wait_ge(dve_y2, NT * (b + 1))
                layer_norm(back, 1, res, x2, dve_x2)

            def qk_halves1(b):
                dve.wait_ge(act_qkv, 3 * b + 1)
                ve.tensor_tensor(q1[64:P, :], ps[64:P, 6, :], q1[64:P, :].bitcast(FP32),
                                 ALU.subtract).then_inc(dve_q1, 1)
                dve.wait_ge(act_qkv, 3 * b + 2)
                ve.tensor_copy(k1b[64:P, :], ps[64:P, 5, :])
                back.link(ve.tensor_tensor(k1b[0:64, :], ps[0:64, 5, :], k1a[0:64, :].bitcast(FP32),
                                           ALU.subtract))
                ve.tensor_tensor(k1a[64:P, :], ps[64:P, 5, :], k1a[64:P, :].bitcast(FP32),
                                 ALU.subtract).then_inc(dve_k1, 1)

            def maximum1(b, t):
                dve.wait_ge(pe_s1, NT * b + t + 1)
                back.link(ve.tensor_reduce(nmax1[:, 0, t:t + 1], ps[:, 5, 0:(t + 1) * P], axis=AX.X, op=ALU.max,
                                           negate=True))
                ve.tensor_scalar(nmax1[:, 1, t:t + 1], nmax1[:, 0, t:t + 1], SCALE1, None,
                                 ALU.mult).then_inc(dve_m1, 1)

            def probs_out1(b, t):
                dve.wait_ge(pe_pT, NT * b + t + 1)
                if t:
                    dve.wait_ge(pe_av1, NT * b + t)
                n = (t + 1) * P
                ve.tensor_copy(probT1[:, 0:n], ps[:, 6, 0:n]).then_inc(dve_pT, 1)

            def attend1(b, t):
                dve.wait_ge(act_p1, NT * b + t + 1)
                back.link(ve.reciprocal(den1[:, 1, t:t + 1], den1[:, 0, t:t + 1]))
                dve.wait_ge(pe_av1, NT * b + t + 1)
                ve.scalar_tensor_tensor(res[:, t, :], ps[:, 5, 0:D], den1[:, 1, t:t + 1], x2[:, t, :],
                                        ALU.mult, ALU.add).then_inc(dve_r3, 1)

            def norm_x3(b):
                dve.wait_ge(dve_r3, NT * (b + 1))
                layer_norm(back, 1, res, x3, dve_x3)

            def x3_lower(b):
                dve.wait_ge(act_x3, 1 * b + 1)
                ve.tensor_tensor(x3_lo[:], ps[:, 6, :], x3_hi[:].bitcast(FP32), ALU.subtract).then_inc(dve_x3lo, 1)

            def angle(b, f):
                dve.wait_ge(act_h1, NF * b + f + 1)
                a, n = ang[:, f % 2, :], ang_n[:]
                back.link(ve.tensor_scalar(a, hid1[:, f % 2, :], 0.1 / TWO_PI, th[:, 2, f:f + 1],
                                           ALU.mult, ALU.add))
                back.link(ve.tensor_scalar(n, a, ROUND, ROUND, ALU.add, ALU.subtract))
                ve.tensor_tensor(a, a, n, ALU.subtract).then_inc(dve_ang, 1)

            def activate(b, f):
                dve.wait_ge(act_sin, NF * b + f + 1)
                back.link(ve.scalar_tensor_tensor(actT[:, f, :], ang[:, f % 2, :], th[:, 1, f:f + 1],
                                                  hid1[:, f % 2, :], ALU.mult, ALU.add))
                ve.tensor_scalar(actT[:, f, :], actT[:, f, :], 0.0, None, ALU.max).then_inc(dve_act, 1)

            def norm_out(b):
                dve.wait_ge(pe_y, 1 * b + 1)
                dve.wait_ge(pool_x3, 1 * b + 1)
                back.link(ve.tensor_tensor(res[:].rearrange("p t d -> p (t d)"), ps[:, 5, :],
                                           x3[:].rearrange("p t d -> p (t d)"), ALU.add))
                dve.wait_ge(y_out, 16 * b + 1)
                layer_norm(back, 1, res, y, dve_y)
                back.end()

            def prepare():
                k = [1]

                def step(ins):
                    k[0] += 1
                    ins.then_inc(w_dve, 1)
                    dve.wait_ge(w_dve, k[0])

                step(ve.tensor_scalar(th[:, 6, :], theta_c, 1.0 / TWO_PI, None, ALU.mult))
                step(ve.tensor_scalar(th[:, 6, :], th[:, 6, :], ROUND, ROUND, ALU.add, ALU.subtract))
                step(ve.scalar_tensor_tensor(th[:, 7, :], th[:, 6, :], -PI_C1, theta_c, ALU.mult, ALU.add))
                step(ve.scalar_tensor_tensor(th[:, 7, :], th[:, 6, :], -PI_C2, th[:, 7, :], ALU.mult, ALU.add))
                step(ve.tensor_scalar(th[:, 7, :], th[:, 7, :], 1.0 / TWO_PI, 0.5, ALU.mult, ALU.min))
                step(ve.tensor_scalar(th[:, 2, :], th[:, 7, :], -0.5, None, ALU.max))
                step(ve.tensor_scalar(th[:, 7, :], th[:, 2, :], 0.25, None, ALU.add))
                step(ve.tensor_scalar(th[:, 6, :], th[:, 7, :], ROUND, ROUND, ALU.add, ALU.subtract))
                step(ve.tensor_tensor(th[:, 3, :], th[:, 7, :], th[:, 6, :], ALU.subtract))
                assert k[0] == W_TURNS
                dve.wait_ge(w_act, 1)
                step(ve.tensor_tensor(th[:, 6, :], th[:, 5, :], w_real_c, ALU.mult))
                step(ve.tensor_tensor(th[:, 7, :], th[:, 4, :], w_imag_c, ALU.mult))
                step(ve.tensor_tensor(th[:, 6, :], th[:, 6, :], th[:, 7, :], ALU.add))
                step(ve.scalar_tensor_tensor(th[:, 1, :], th[:, 6, :], 0.1, w_imag_c, ALU.mult, ALU.mult))

            def middle(b):
                norm_z(b)
                norm_x1(b)
                x1_lower(b)
                gate_logits(b)
                gate_weights(b)

            ve.memset(qstack[64:P].rearrange("p h n -> p (h n)").bitcast(FP32), 0.0)
            ve.memset(kstack[64:P].rearrange("p h n -> p (h n)").bitcast(FP32), 0.0).then_inc(w_zero, 1)
            dve.wait_ge(w_zero, 1)
            ve.memset(kstack[ROWS:ROWS + PARTS], 1.0).then_inc(w_zero, 1)
            dve.wait_ge(w_in, 16 * N_SMALL)
            dve.wait_ge(w_pe, 1)
            ve.tensor_copy(vecs[:], ps[:, 5, 0:N_VEC]).then_inc(w_dve, 1)
            dve.wait_ge(w_dve, 1)
            parts(0)
            for j in range(NG):
                maxima(0, j)
            max_parts(0)
            prepare()
            for t in range(NT):
                divide(0, t)
            middle(0)
            for m in range(NM):
                expert_hidden(0, m)
            with dve.Fori(1, B) as b:
                parts(b)
                for j in range(NG):
                    maxima(b, j)
                    if j % 11 == 10 and j > 11:
                        mix(b - 1, j // 11 - 1)
                mix(b - 1, NT - 1)
                max_parts(b)
                norm_x2(b - 1)
                qk_halves1(b - 1)
                for t in range(NT):
                    maximum1(b - 1, t)
                    probs_out1(b - 1, t)
                    attend1(b - 1, t)
                norm_x3(b - 1)
                for t in range(NT):
                    divide(b, t)
                norm_z(b)
                x3_lower(b - 1)
                norm_x1(b)
                x1_lower(b)
                gate_logits(b)
                gate_weights(b)
                for m in range(NM):
                    expert_hidden(b, m)
                    if m % 5 == 2 and m // 5 < NF:
                        angle(b - 1, m // 5)
                    if m % 5 == 4 and m // 5 < NF:
                        activate(b - 1, m // 5)
                norm_out(b - 1)
            last_b = B - 1
            for t in range(NT):
                mix(last_b, t)
            norm_x2(last_b)
            qk_halves1(last_b)
            for t in range(NT):
                maximum1(last_b, t)
                probs_out1(last_b, t)
                attend1(last_b, t)
            norm_x3(last_b)
            x3_lower(last_b)
            for f in range(NF):
                angle(last_b, f)
                if f:
                    activate(last_b, f - 1)
            activate(last_b, NF - 1)
            norm_out(last_b)


_INS = ['L0_attn_x', 'L0_attn_Wq', 'L0_attn_bq', 'L0_attn_Wk', 'L0_attn_bk', 'L0_attn_Wv', 'L0_attn_bv',
        'L0_attn_ln_g', 'L0_attn_ln_b', 'L0_attn_Wo', 'L0_attn_bo', 'L0_ffn_gate_w', 'L0_ffn_w1', 'L0_ffn_w2',
        'L0_ffn_w3', 'L1_attn_Wq', 'L1_attn_Wk', 'L1_attn_Wv', 'L1_ffn_W1', 'L1_ffn_b1',
        'L1_ffn_quantum_phases', 'L1_ffn_quantum_weights_real', 'L1_ffn_quantum_weights_imag', 'L1_ffn_W2',
        'L1_ffn_b2']


def kernel(**inputs):
    import concourse.bacc as _bacc
    from concourse.bass_utils import run_bass_kernel_spmd as _run

    nc = _bacc.Bacc("TRN2", target_bir_lowering=False, num_devices=1)
    arrays, args = {}, []
    for name in _INS:
        a = np.ascontiguousarray(inputs[name])
        arrays[f"in_{name}"] = a
        args.append(nc.dram_tensor(f"in_{name}", a.shape, mybir.dt.from_np(a.dtype), kind="ExternalInput").ap())
    args.append(nc.dram_tensor("out_0", (B, S, D), FP32, kind="ExternalOutput").ap())
    build(nc, *args)
    r = _run(nc, [arrays], core_ids=[0])
    return r.results[0]["out_0"]
```

```python
from contextlib import ExitStack

import numpy as np

import concourse.bass as bass
from concourse import mybir

FP32 = mybir.dt.float32
FP32R = mybir.dt.float32r
BF16 = mybir.dt.bfloat16
I32 = mybir.dt.int32
ALU = mybir.AluOpType
ACT = mybir.ActivationFunctionType
AX = mybir.AxisListType

P = 128
B, S, D = 4, 512, 128
NT = S // P
H, G, HD = 4, 4, 8
NH = H * G
KV = H * HD
PARTS = 3
TERMS = PARTS * PARTS
ROWS = 96
E, FF0 = 4, 704
FULL = FF0 // P
TAIL = FF0 - FULL * P
NM = E * FF0 // P
DQ = 64
FF1 = 512
NF = FF1 // P
EPS = 1e-5
NEG = -1e30
SCALE0 = float(HD) ** -0.5
SCALE1 = float(DQ) ** -0.5
TWO_PI = 2.0 * np.pi
PI_C1 = 6.28125
PI_C2 = float(np.float32(TWO_PI - PI_C1))
TURN = float(np.nextafter(np.float32(TWO_PI), np.float32(0)))
ROUND = 1.5 * 2.0 ** 23
RSQRT_SEED = float(0x5F3759DF)

MAX_GROUPS = [(qt, h0, hn) for qt, hn in ((0, 4), (1, 2), (2, 1), (3, 1)) for h0 in range(0, NH, hn)]
UNITS = [[(0, h, 0, 0), (3, h, 512, 384), (1, h, 640, 128)] for h in range(H)]
UNITS.append([(2, h, 256 * h, 256) for h in range(H)])
NU = len(UNITS)
PLACE = {(kb, h): (u, col, q0) for u, unit in enumerate(UNITS) for kb, h, col, q0 in unit}
MAX_BANKS = (4, 7, 0, 1, 2, 3)
GROUPS1 = [(0, 2), (2, 1), (3, 1)]
NB1 = len(GROUPS1)
EXPERT_TILES = [[FULL * e + j for j in range(FULL)] + [E * FULL + e // 2] for e in range(E)]


W_TURNS = 10
N_FRONT = 49
N_BACK = 63
N_PARTS = 8
S1, T1, V1, A1 = (1, 1, 11), (6, 6, 14), (9, 9, 18), (3, 4, 13)
N_VEC = 4 * NF + E + 4


def tiles_of(dst, src):
    pairs = [(dst[:, 0:E * FULL, :].rearrange("p (e n) c -> p e (n c)", e=E), src[:, :, 0:FULL * P])]
    for m in range(E // 2):
        pairs.append((dst[:, E * FULL + m, :].rearrange("p (e c) -> p e c", e=2),
                      src[:, 2 * m:2 * m + 2, FULL * P:FF0]))
    return pairs


class Chain:

    def __init__(self, eng, sem, per):
        self.eng, self.sem, self.per = eng, sem, per

    def begin(self, b, n=0):
        self.base, self.n = b * self.per, n

    def link(self, ins):
        self.n += 1
        ins.then_inc(self.sem, 1)
        self.eng.wait_ge(self.sem, self.base + self.n)

    def pause(self):
        assert self.n == N_PARTS, self.n

    def end(self):
        assert self.n == self.per, (self.n, self.per)


def build(nc, x, Wq0, bq0, Wk0, bk0, Wv0, bv0, ln_g, ln_b, Wo0, bo0, gate_w, w1, w2, w3,
          Wq1, Wk1, Wv1, fW1, fb1, theta, w_real, w_imag, fW2, fb2, out):
    ctx = ExitStack()
    with ctx:
        def sb(name, shape, dt=FP32):
            return ctx.enter_context(nc.sbuf_tensor(name, shape, dt))

        def sem(name):
            return ctx.enter_context(nc.semaphore(name))

        ident = sb("ident", [P, P])
        ident_h = sb("ident_h", [P, P], BF16)
        future_h = sb("future_h", [P, 4, P], BF16)
        before = sb("before", [P, E, E])
        wq0 = sb("wq0", [P, D])
        wk0 = sb("wk0", [P, KV])
        wv0 = sb("wv0", [P, KV])
        wo0 = sb("wo0", [P, D])
        vec_rows = sb("vec_rows", [N_VEC, P])
        vecs = sb("vecs", [P, N_VEC])
        theta_c, w_real_c, w_imag_c, fb1_c = (vecs[:, NF * n:NF * (n + 1)] for n in range(4))
        gateT = vecs[:, 4 * NF:4 * NF + E]
        bq_c, lng_c, lnb_c, bk_c = (vecs[:, 4 * NF + E + n:4 * NF + E + n + 1] for n in range(4))
        bv_r = sb("bv_r", [P, KV])
        bo_r = sb("bo_r", [P, D])
        b2_r = sb("b2_r", [P, D])
        up_hi = [sb(f"up{n}_hi", [P, NM, P], FP32R) for n in range(2)]
        up_lo = [sb(f"up{n}_lo", [P, NM, P], FP32R) for n in range(2)]
        down = sb("down", [P, E * (FULL + 1), D])
        wq1 = sb("wq1", [P, 2, DQ])
        wk1 = sb("wk1", [P, 2, DQ])
        wv1 = sb("wv1", [P, D])
        f1 = sb("f1", [P, FF1])
        f1_hi = sb("f1_hi", [P, FF1], FP32R)
        f1_lo = sb("f1_lo", [P, FF1], FP32R)
        f2 = sb("f2", [P, NF, D])
        th = sb("th", [P, 8, NF])
        xin = sb("xin", [P, NT, D])
        xres = sb("xres", [P, NT, D])
        xT = sb("xT", [P, S])
        part_f = sb("part_f", [P, S])
        zT = part_f
        qparts = sb("qparts", [P, PARTS, S], BF16)
        kparts = sb("kparts", [KV, PARTS, S], BF16)
        qstack = sb("qstack", [P, NH, S], BF16)
        kstack = sb("kstack", [P, H, S], BF16)
        vext = sb("vext", [P, NT, H, 32])
        negmax = sb("negmax", [P, NT, NH])
        mrow = sb("mrow", [NH, S])
        mparts = sb("mparts", [NH, PARTS, S], BF16)
        hidT = sb("hidT", [P, NM, S])
        flat = hidT[:].rearrange("p a b -> p (a b)")
        probs = flat[:, 0:2 * NU * 1024].rearrange("p (a u n) -> p a u n", a=2, u=NU)
        stage = flat[:, 0:2 * E * FF0].rearrange("p (w e n) -> p w e n", w=2, e=E)
        uT = sb("uT", [P, G, S])
        rden0 = sb("rden0", [P, NT, NH])
        att = sb("att", [P, NT, D])
        attn = xT[:].rearrange("p (t d) -> p t d", t=NT)
        res1 = att
        x1 = sb("x1", [P, NT, D])
        x1T = sb("x1T", [P, S])
        x1_hi = sb("x1_hi", [P, S], FP32R)
        x1_lo = sb("x1_lo", [P, S], FP32R)
        lg = sb("lg", [P, NT, E])
        lgx = sb("lgx", [P, 4, NT, E])
        cmp4 = sb("cmp4", [P, 2, NT, E, E])
        lgs = sb("lgs", [P, NT])
        cw = sb("cw", [P, NT, E])
        silu = sb("silu", [P, 2, S])
        res = sb("res", [P, NT, D])
        x2 = sb("x2", [P, NT, D])
        two_a = sb("two_a", [P, 2, S])
        x2T = two_a[:, 0, :]
        v1 = two_a[:, 1, :].rearrange("p (t d) -> p t d", t=NT)
        hid1 = two_a
        two_b = sb("two_b", [P, 2, S])
        ang = two_b
        ang_n = sb("ang_n", [P, S])
        prob1 = (two_b[:, 0, :], ang_n[:], two_b[:, 0, :])
        probT1 = (two_b[:, 1, :], two_a[:, 0, :], two_b[:, 1, :])
        q1 = sb("q1", [P, S], FP32R)
        k1a = sb("k1a", [P, S], FP32R)
        k1b = sb("k1b", [P, S], FP32R)
        x3_hi, x3_lo = q1, k1a
        nmax1 = sb("nmax1", [P, 2, NT])
        den1 = sb("den1", [P, 2, NT])
        x3 = sb("x3", [P, NT, D])
        actT = uT
        y = sb("y", [P, NT, D])
        carry = sb("carry", [P, 1 + G * NU])
        stats = [sb(f"stats{n}", [P, NT, 6]) for n in range(2)]
        mv = [sb(f"mv{n}", [P, NT, 2]) for n in range(2)]
        ln_s = [sb(f"ln_s{n}", [P, 4, NT]) for n in range(2)]

        ps = ctx.enter_context(nc.psum_tensor("ps", [P, 8, 512], FP32))
        q_scr = nc.dram_tensor("q_scr", (PARTS, D, S), BF16, kind="Internal").ap()
        k_scr = nc.dram_tensor("k_scr", (PARTS, KV, S), BF16, kind="Internal").ap()
        m_scr = nc.dram_tensor("m_scr", (PARTS, NH, S), BF16, kind="Internal").ap()

        w_in = sem("w_in")
        w_up_in = sem("w_up_in")
        w_down_in = sem("w_down_in")
        w_pool = sem("w_pool")
        w_zero = sem("w_zero")
        w_dve = sem("w_dve")
        w_act = sem("w_act")
        w_hi = sem("w_hi")
        w_lo = sem("w_lo")
        w_pe = sem("w_pe")
        x_in = sem("x_in")
        x_res = sem("x_res")
        qk_out = sem("qk_out")
        qk_in = sem("qk_in")
        m_out = sem("m_out")
        m_in = sem("m_in")
        y_out = sem("y_out")
        pe_proj = sem("pe_proj")
        pe_max = sem("pe_max")
        pe_mrow = sem("pe_mrow")
        pe_unit = sem("pe_unit")
        pe_av = sem("pe_av")
        pe_o = sem("pe_o")
        pe_tail = sem("pe_tail")
        pe_up = sem("pe_up")
        act_xT = sem("act_xT")
        act_exp = sem("act_exp")
        act_uT = sem("act_uT")
        act_zT = sem("act_zT")
        act_x1T = sem("act_x1T")
        act_gate = sem("act_gate")
        act_silu = sem("act_silu")
        pool_mask = sem("pool_mask")
        dve_part = sem("dve_part")
        dve_qk = sem("dve_qk")
        dve_max = sem("dve_max")
        dve_mrow = sem("dve_mrow")
        dve_o = sem("dve_o")
        dve_z = sem("dve_z")
        dve_wo = sem("dve_wo")
        dve_x1 = sem("dve_x1")
        dve_x1lo = sem("dve_x1lo")
        dve_lg = sem("dve_lg")
        dve_cw = sem("dve_cw")
        dve_hid = sem("dve_hid")
        ch0 = sem("ch0")
        pe_down = sem("pe_down")
        pe_x2 = sem("pe_x2")
        pe_s1 = sem("pe_s1")
        pe_pT = sem("pe_pT")
        pe_av1 = sem("pe_av1")
        pe_x3 = sem("pe_x3")
        pe_h1 = sem("pe_h1")
        pe_y = sem("pe_y")
        act_x2T = sem("act_x2T")
        act_qkv = sem("act_qkv")
        act_p1 = sem("act_p1")
        act_x3 = sem("act_x3")
        act_h1 = sem("act_h1")
        act_sin = sem("act_sin")
        act_relu = sem("act_relu")
        pool_x3 = sem("pool_x3")
        dve_y2 = sem("dve_y2")
        dve_x2 = sem("dve_x2")
        dve_q1 = sem("dve_q1")
        dve_k1 = sem("dve_k1")
        dve_m1 = sem("dve_m1")
        dve_pT = sem("dve_pT")
        dve_r3 = sem("dve_r3")
        dve_x3 = sem("dve_x3")
        dve_x3lo = sem("dve_x3lo")
        dve_ang = sem("dve_ang")
        dve_act = sem("dve_act")
        dve_y = sem("dve_y")
        ch1 = sem("ch1")
        NG = len(MAX_GROUPS)
        NQ = G * NU

        block = ctx.enter_context(nc.Block())

        x_v = x.rearrange("b (t p) d -> b p t d", p=P)
        out_v = out.rearrange("b (t p) d -> b p t d", p=P)

        def row(ap, n):
            return ap.rearrange("(a n) -> a n", a=1).to_broadcast([P, n])


        N_SMALL = 23
        Z_DOWN, Z_CONST = 2, 8

        def first(b):
            return isinstance(b, int) and b == 0

        @block.sync
        def _(sp):
            loads = []

            def load(dst, src):
                loads.append(sp.dma_start(dst, src).then_inc(w_in, 16))

            def load_x(b):
                if not first(b):
                    sp.wait_ge(x_res, 1 * b)
                sp.dma_start(xin[:], x_v[bass.ds(b, 1)].rearrange("a p t d -> p (a t) d")).then_inc(x_in, 16)

            def restack(b):
                sp.wait_ge(dve_qk, 2 * b + 1)
                sp.dma_start(q_scr.rearrange("a p n -> p a n"), qparts[:]).then_inc(qk_out, 16)
                sp.wait_ge(dve_qk, 2 * b + 2)
                sp.dma_start(k_scr.rearrange("a p n -> p a n"), kparts[:]).then_inc(qk_out, 16)
                sp.wait_ge(qk_out, 32 * b + 32)
                for t in range(TERMS):
                    for dst, src, part in ((kstack, k_scr, t % PARTS), (qstack, q_scr, t // PARTS)):
                        sp.dma_start(dst[HD * t:HD * (t + 1)],
                                     src[part].rearrange("(h d) n -> d h n", d=HD)).then_inc(qk_in, 16)

            def restack_max(b):
                sp.wait_ge(dve_mrow, 2 * b + 2)
                sp.dma_start(m_scr.rearrange("a h n -> h a n"), mparts[:]).then_inc(m_out, 16)
                sp.wait_ge(m_out, 16 * b + 16)
                sp.dma_start(qstack[ROWS:ROWS + PARTS], m_scr).then_inc(m_in, 16)

            def store(b):
                sp.wait_ge(dve_y, 1 * b + 1)
                sp.dma_start(out_v[bass.ds(b, 1)].rearrange("a p t d -> p (a t) d"), y[:]).then_inc(y_out, 16)

            load_x(0)
            sp.wait_ge(w_pool, 1)
            for n, v in enumerate((theta, w_real, w_imag, fb1)):
                load(vec_rows[NF * n:NF * (n + 1), :], v.rearrange("(f p) -> f p", p=P))
            load(vec_rows[4 * NF:4 * NF + E, :], gate_w[0:E, :])
            for n, v in enumerate((bq0, ln_g, ln_b, bk0)):
                k = 4 * NF + E + n
                load(vec_rows[k:k + 1, 0:v.shape[0]], v.rearrange("(a n) -> a n", a=1))
            load(wq0[:], Wq0)
            load(wk0[:], Wk0)
            load(wv0[:], Wv0)
            load(bv_r[:], row(bv0, KV))
            load(bo_r[:], row(bo0, D))
            load(wo0[:], Wo0)
            load(f1[:], fW1)
            load(b2_r[:], row(fb2, D))
            load(wv1[:], Wv1)
            for half in range(2):
                load(wq1[:, half, :], Wq1)
                load(wk1[:, half, :], Wk1)
            load(f2[:], fW2.rearrange("(f p) d -> p f d", p=P))
            assert len(loads) == N_SMALL, len(loads)
            sp.dma_start(stage[:, 0], w1[0:E].rearrange("e d n -> d e n")).then_inc(w_up_in, 16)
            sp.dma_start(stage[:, 1], w3[0:E].rearrange("e d n -> d e n")).then_inc(w_up_in, 16)
            sp.wait_ge(w_zero, 2)
            restack(0)
            sp.wait_ge(w_pool, Z_DOWN)
            for e in range(E):
                n0 = e * (FULL + 1)
                sp.dma_start(down[:, n0:n0 + FULL, :],
                             w2[e, 0:FULL * P, :].rearrange("(j p) d -> p j d", p=P)).then_inc(w_down_in, 16)
                p0 = TAIL * (e % 2)
                sp.dma_start(down[p0:p0 + TAIL, n0 + FULL, :], w2[e, FULL * P:, :]).then_inc(w_down_in, 16)
            def element(b, more):
                if more:
                    load_x(b + 1)
                restack_max(b)
                if more:
                    restack(b + 1)

            element(0, True)
            with sp.Fori(1, B - 1) as b:
                element(b, True)
                store(b - 1)
            element(B - 1, False)
            store(B - 2)
            store(B - 1)
            sp.wait_ge(y_out, 16 * B + 1)

        @block.gpsimd
        def _(pool):
            gp = nc.gpsimd
            gp.memset(vec_rows[:], 0.0).then_inc(w_pool, 1)
            gp.memset(down[:, FULL::FULL + 1, :], 0.0).then_inc(w_pool, 1)
            pool.wait_ge(w_pool, 1)
            gp.memset(ident[:], 0.0)
            gp.memset(future_h[:], 0.0)
            gp.memset(before[:], 1.0)
            gp.memset(carry[:], 0.0)
            gp.memset(vext[:], 0.0).then_inc(w_pool, 1)
            pool.wait_ge(w_pool, 3)
            gp.affine_select(out=ident[:], in_=ident[:], compare_op=ALU.not_equal, fill=1.0, base=0,
                             pattern=[[-1, P]], channel_multiplier=1).then_inc(w_pool, 1)
            gp.affine_select(out=future_h[:], in_=future_h[:], compare_op=ALU.is_ge, fill=NEG, base=0,
                             pattern=[[0, 4], [-1, P]], channel_multiplier=1).then_inc(w_pool, 1)
            gp.affine_select(out=before[:], in_=before[:], compare_op=ALU.is_gt, fill=0.0, base=0,
                             pattern=[[1, E], [-1, E]], channel_multiplier=0).then_inc(w_pool, 1)
            gp.memset(vext[:, :, :, HD:HD + 1], 1.0).then_inc(w_pool, 1)
            pool.wait_ge(w_pool, 4)
            gp.tensor_copy(ident_h[:], ident[:]).then_inc(w_pool, 1)
            gp.memset(y[:, 0, 0:1], 0.0).then_inc(y_out, 1)

            def residual_x(b):
                pool.wait_ge(pe_proj, 4 * b + 1)
                gp.tensor_tensor(xres[:], xin[:], bo_r[:].unsqueeze(1).to_broadcast([P, NT, D]),
                                 ALU.add).then_inc(x_res, 1)

            def masks(b):
                for g in range(G):
                    for u in range(NU):
                        n = NU * g + u
                        pool.wait_ge(act_exp, NQ * b + n + 1)
                        gp.tensor_tensor(carry[:, n + 1:n + 2], carry[:, 0:1], carry[:, 0:1], ALU.add)
                        pr = probs[:, g % 2, u, :]
                        if u < H:
                            spots = [(pr[:, 0:P], [[1, P]]),
                                     (pr[:, 512:512 + 2 * P].rearrange("p (a q) -> p a q", a=2), [[0, 2], [1, P]])]
                        else:
                            spots = [(pr.rearrange("p (a q) -> p a q", a=H)[:, :, 0:P], [[0, H], [1, P]])]
                        for spot, pattern in spots:
                            last = gp.affine_select(out=spot, in_=spot, compare_op=ALU.is_ge, fill=0.0, base=0,
                                                    pattern=pattern, channel_multiplier=-1)
                        last.then_inc(pool_mask, 1)

            def residual_x3(b):
                pool.wait_ge(pe_x3, 1 * b + 1)
                gp.tensor_tensor(x3[:], x3[:], b2_r[:].unsqueeze(1).to_broadcast([P, NT, D]),
                                 ALU.add).then_inc(pool_x3, 1)

            pool.wait_ge(w_in, 16 * N_SMALL)
            residual_x(0)
            for n, (hi, lo) in enumerate(zip(up_hi, up_lo)):
                for k, (dst, src) in enumerate(tiles_of(lo, stage[:, n])):
                    pool.wait_ge(w_hi, 3 * n + k + 1)
                    gp.tensor_tensor(dst, src, tiles_of(hi, stage[:, n])[k][0].bitcast(FP32),
                                     ALU.subtract).then_inc(w_lo, 1)
            pool.wait_ge(w_hi, 7)
            gp.tensor_tensor(f1_lo[:], f1[:], f1_hi[:].bitcast(FP32), ALU.subtract).then_inc(w_lo, 1)
            masks(0)
            residual_x(1)
            with pool.Fori(1, B - 1) as b:
                masks(b)
                residual_x3(b - 1)
                residual_x(b + 1)
            masks(B - 1)
            residual_x3(B - 2)
            residual_x3(B - 1)

        @block.scalar
        def _(act):
            sc = nc.scalar

            def xT_out(b):
                act.wait_ge(pe_proj, 4 * b + 1)
                if not first(b):
                    act.wait_ge(pe_proj, 4 * b)
                sc.activation(xT[:], ps[:, 4, :], ACT.Copy).then_inc(act_xT, 1)

            def exps(b, n):
                g, u = n // NU, n % NU
                act.wait_ge(pe_unit, NQ * b + n + 1)
                if n == 0 and first(b):
                    act.wait_ge(w_lo, 7)
                if g < 2:
                    if u == 0 and not first(b):
                        act.wait_ge(pe_down, NT * b)
                else:
                    act.wait_ge(pe_av, G * b + g - 1)
                pair = 2 * (n % 2)
                sc.activation(probs[:, g % 2, u, :].rearrange("p (a n) -> p a n", a=2),
                              ps[:, pair:pair + 2, :], ACT.Exp, scale=SCALE0).then_inc(act_exp, 1)

            def uT_out(b, g):
                act.wait_ge(pe_av, G * b + g + 1)
                if g == 0 and not first(b):
                    act.wait_ge(pe_o, NT * b)
                sc.activation(uT[:, g, :], ps[:, (7, 4)[g % 2], :], ACT.Copy).then_inc(act_uT, 1)

            def zT_out(b):
                act.wait_ge(pe_tail, 4 * b + 1)
                sc.activation(zT[:], ps[:, 7, :], ACT.Identity, bias=lnb_c,
                              scale=lng_c).then_inc(act_zT, 1)

            def x1T_out(b):
                act.wait_ge(pe_tail, 4 * b + 3)
                if not first(b):
                    act.wait_ge(pe_up, 2 * NM * b)
                    act.wait_ge(dve_x1lo, 1 * b)
                sc.activation(x1T[:], ps[:, 7, :], ACT.Copy).then_inc(act_x1T, 1)
                sc.activation(x1_hi[:], ps[:, 7, :], ACT.Copy).then_inc(act_x1T, 1)

            def gate_tanh(b):
                act.wait_ge(dve_lg, 2 * b + 2)
                sc.activation(lgx[:, 3], lgx[:, 2], ACT.Tanh).then_inc(act_gate, 1)

            def silus(b, m):
                act.wait_ge(pe_up, 2 * NM * b + 2 * m + 1)
                if not (first(b) and m < 2):
                    act.wait_ge(dve_hid, NM * b + m - 1)
                sc.activation(silu[:, m % 2, :], ps[:, 2 * (m % 2), :], ACT.Silu).then_inc(act_silu, 1)

            def x2T_out(b):
                act.wait_ge(pe_x2, 4 * b + 1)
                sc.activation(x2T[:], ps[:, 5, :], ACT.Copy).then_inc(act_x2T, 1)

            def qkv1_out(b):
                act.wait_ge(pe_x2, 4 * b + 2)
                sc.activation(q1[:], ps[:, 6, :], ACT.Copy).then_inc(act_qkv, 1)
                act.wait_ge(pe_x2, 4 * b + 3)
                sc.activation(k1a[:], ps[:, 5, :], ACT.Copy).then_inc(act_qkv, 1)

            def v1_out(b):
                act.wait_ge(pe_x2, 4 * b + 4)
                sc.activation(two_a[:, 1, :], ps[:, 6, :], ACT.Copy).then_inc(act_qkv, 1)

            def exp1(b, n):
                t0, nt = GROUPS1[n]
                act.wait_ge(dve_m1, NB1 * b + n + 1)
                if n == 2:
                    act.wait_ge(pe_pT, NB1 * b + 1)
                col = 0
                for t in range(t0, t0 + nt):
                    w = (t + 1) * P
                    last = sc.activation(prob1[n][:, col:col + w], ps[:, 5 + n % 2, col:col + w], ACT.Exp,
                                         bias=nmax1[:, 1, t:t + 1], scale=SCALE1,
                                         accum_out=den1[:, 0, t:t + 1])
                    col += w
                last.then_inc(act_p1, 1)

            def x3_out(b):
                act.wait_ge(pe_x3, 1 * b + 1)
                sc.activation(x3_hi[:], ps[:, 6, :], ACT.Copy).then_inc(act_x3, 1)

            def hidden1_out(b, f):
                act.wait_ge(pe_h1, NF * b + f + 1)
                if f >= 2:
                    act.wait_ge(dve_act, NF * b + f - 1)
                sc.activation(hid1[:, f % 2, :], ps[:, 5 + f % 2, :], ACT.Identity, bias=fb1_c[:, f:f + 1])
                sc.activation(ang[:, f % 2, :], ps[:, 5 + f % 2, :], ACT.Identity, bias=th[:, 0, f:f + 1],
                              scale=0.1 / TWO_PI).then_inc(act_h1, 1)

            def sines(b, f):
                act.wait_ge(dve_ang, NF * b + f + 1)
                sc.activation(ang[:, f % 2, :], ang[:, f % 2, :], ACT.Sin, scale=TURN).then_inc(act_sin, 1)

            def rectify(b, f):
                act.wait_ge(dve_act, NF * b + f + 1)
                sc.activation(actT[:, f, :], actT[:, f, :], ACT.Relu).then_inc(act_relu, 1)

            xT_out(0)
            act.wait_ge(w_up_in, 32)
            for n, hi in enumerate(up_hi):
                for dst, src in tiles_of(hi, stage[:, n]):
                    sc.activation(dst, src, ACT.Copy).then_inc(w_hi, 1)
            sc.activation(f1_hi[:], f1[:], ACT.Copy).then_inc(w_hi, 1)
            act.wait_ge(w_dve, W_TURNS)
            sc.activation(th[:, 4:6, :], th[:, 2:4, :], ACT.Sin, scale=TURN).then_inc(w_act, 1)

            def element(b, more, back):
                prev = b - 1
                if back:
                    x2T_out(prev)
                    qkv1_out(prev)
                    v1_out(prev)
                for n in range(NQ):
                    exps(b, n)
                    if n % NU == 2 and n > NU:
                        uT_out(b, n // NU - 1)
                    if back and n in (A1[0], A1[1], A1[2]):
                        exp1(prev, A1.index(n))
                uT_out(b, G - 1)
                if back:
                    x3_out(prev)
                    hidden1_out(prev, 0)
                    hidden1_out(prev, 1)
                zT_out(b)
                if back:
                    for f in range(2):
                        sines(prev, f)
                    for f in range(2):
                        rectify(prev, f)
                        hidden1_out(prev, f + 2)
                x1T_out(b)
                if back:
                    for f in range(2, NF):
                        sines(prev, f)
                    for f in range(2, NF):
                        rectify(prev, f)
                for m in range(NM):
                    silus(b, m)
                    if m == 3:
                        gate_tanh(b)
                    if m == 4 and more:
                        xT_out(b + 1)

            element(0, True, False)
            with act.Fori(1, B - 1) as b:
                element(b, True, True)
            element(B - 1, False, True)
            last = B - 1
            x2T_out(last)
            qkv1_out(last)
            v1_out(last)
            for n in range(NB1):
                exp1(last, n)
            x3_out(last)
            hidden1_out(last, 0)
            hidden1_out(last, 1)
            for f in range(NF):
                sines(last, f)
                rectify(last, f)
                if f + 2 < NF:
                    hidden1_out(last, f + 2)

        @block.tensor
        def _(pe):
            last_b = B - 1
            mm, tr = nc.tensor.matmul, nc.tensor.transpose

            def split3(dst, hi, lo, vhi, vlo):
                mm(dst, hi, vhi, start=True, stop=False)
                mm(dst, hi, vlo, start=False, stop=False)
                return mm(dst, lo, vhi, start=False, stop=True)

            def cols(t):
                return slice(t * P, (t + 1) * P)

            def project(b):
                pe.wait_ge(x_in, 16 * b + 16)
                if not first(b):
                    pe.wait_ge(dve_lg, 2 * b)
                for t in range(NT):
                    last = tr(ps[:, 4, cols(t)], xin[:, t, :], ident[:])
                last.then_inc(pe_proj, 1)

            def project_qk(b):
                pe.wait_ge(act_xT, 1 * b + 1)
                mm(ps[:, 7, :], wq0[:], xT[:], start=True, stop=True).then_inc(pe_proj, 1)
                mm(ps[0:KV, 4, :], wk0[:], xT[:], start=True, stop=True).then_inc(pe_proj, 1)

            def project_v(b):
                pe.wait_ge(dve_part, 3 * b + 1)
                for t in range(NT):
                    last = mm(ps[:, 7, KV * t:KV * (t + 1)], xT[:, cols(t)], wv0[:], start=True, stop=True)
                last.then_inc(pe_proj, 1)

            def scores_for_max(b, j):
                qt, h0, hn = MAX_GROUPS[j]
                n, bank = (qt + 1) * P, MAX_BANKS[j % len(MAX_BANKS)]
                if j == 0:
                    pe.wait_ge(qk_in, 32 * TERMS * (b + 1))
                    pe.wait_ge(dve_part, 3 * b + 2)
                elif j == 1:
                    pe.wait_ge(dve_part, 3 * b + 3)
                elif j >= len(MAX_BANKS):
                    pe.wait_ge(dve_max, NG * b + j + 1 - len(MAX_BANKS))
                elif j == 2 and not first(b):
                    pe.wait_ge(dve_hid, NM * b)
                for k in range(hn):
                    dst = ps[:, bank, k * n:(k + 1) * n]
                    mm(dst, qstack[0:ROWS, h0 + k, cols(qt)], kstack[0:ROWS, (h0 + k) % H, 0:n],
                       start=True, stop=False)
                    last = mm(dst[:, qt * P:n], ident_h[:], future_h[:, 0, :], start=False, stop=True)
                last.then_inc(pe_max, 1)

            def transpose_max(b):
                pe.wait_ge(dve_max, NG * (b + 1))
                for t in range(NT):
                    last = tr(ps[0:NH, 4, cols(t)], negmax[:, t, :], ident[:])
                last.then_inc(pe_mrow, 1)

            def exact_unit(b, n):
                g, u = n // NU, n % NU
                pair = 2 * (n % 2)
                if n == 0:
                    pe.wait_ge(m_in, 16 * b + 16)
                if n == 0:
                    pe.wait_ge(dve_max, NG * (b + 1))
                if n >= 2:
                    pe.wait_ge(act_exp, NQ * b + n - 1)
                for kb, h, col, q0 in UNITS[u]:
                    n_q = S - q0
                    last = mm(ps[:, pair + col // 512, col % 512:col % 512 + n_q], kstack[:, h, cols(kb)],
                              qstack[:, H * g + h, q0:S], start=True, stop=True)
                last.then_inc(pe_unit, 1)

            def values(b, g):
                bank = (7, 4)[g % 2]
                pe.wait_ge(pool_mask, NQ * b + NU * (g + 1))
                if g == 0:
                    pe.wait_ge(dve_part, 3 * b + 3)
                elif g == 1:
                    pe.wait_ge(dve_mrow, 2 * b + 1)
                else:
                    pe.wait_ge(act_uT, G * b + g - 1)
                for kb in range(NT):
                    for h in range(H):
                        u, col, q0 = PLACE[kb, h]
                        last = mm(ps[32 * h:32 * h + 32, bank, q0:S], vext[:, kb, h, :],
                                  probs[:, g % 2, u, col:col + S - q0], start=(kb == 0), stop=(kb == NT - 1))
                last.then_inc(pe_av, 1)

            def transpose_o(b, t):
                if t == 0:
                    pe.wait_ge(act_uT, G * (b + 1))
                if t >= 2:
                    pe.wait_ge(dve_o, NT * b + t - 1)
                for g in range(G):
                    last = tr(ps[:, (7, 4)[t % 2], cols(g)], uT[:, g, cols(t)], ident[:])
                last.then_inc(pe_o, 1)

            def transpose_z(b):
                pe.wait_ge(dve_z, 1 * b + 1)
                for t in range(NT):
                    last = tr(ps[:, 7, cols(t)], attn[:, t, :], ident[:])
                last.then_inc(pe_tail, 1)

            def project_out(b):
                pe.wait_ge(act_zT, 1 * b + 1)
                for t in range(NT):
                    last = mm(ps[:, 4, cols(t)], zT[:, cols(t)], wo0[:], start=True, stop=True)
                last.then_inc(pe_tail, 1)

            def transpose_x1(b):
                pe.wait_ge(dve_x1, 1 * b + 1)
                for t in range(NT):
                    last = tr(ps[:, 7, cols(t)], x1[:, t, :], ident[:])
                last.then_inc(pe_tail, 1)

            def gate(b):
                pe.wait_ge(act_x1T, 2 * b + 1)
                for t in range(NT):
                    last = mm(ps[:, 4, E * t:E * (t + 1)], x1T[:, cols(t)], gateT, start=True, stop=True)
                last.then_inc(pe_tail, 1)

            def experts_up(b, m):
                pair = 2 * (m % 2)
                if m == 0:
                    pe.wait_ge(dve_x1lo, 1 * b + 1)
                    pe.wait_ge(act_exp, NQ * (b + 1))
                if m >= 2:
                    pe.wait_ge(dve_hid, NM * b + m - 1)
                for n in range(2):
                    split3(ps[:, pair + n, :], up_hi[n][:, m, :], up_lo[n][:, m, :],
                           x1_hi[:], x1_lo[:]).then_inc(pe_up, 1)

            def experts_down(b, t, e):
                if t == 0 and e == 0:
                    pe.wait_ge(dve_hid, NM * (b + 1))
                    if b is last_b:
                        pe.wait_ge(dve_y, b)
                if t >= 2 and e == 0:
                    pe.wait_ge(dve_y2, NT * b + t - 1)
                for j, tile in enumerate(EXPERT_TILES[e]):
                    last = mm(ps[:, 5 + t % 2, cols(e)], hidT[:, tile, cols(t)],
                              down[:, e * (FULL + 1) + j, :], start=(e == 0 and j == 0),
                              stop=(j == FULL), skip_group_check=True)
                if e == E - 1:
                    last.then_inc(pe_down, 1)

            def project1(b):
                pe.wait_ge(dve_x2, 1 * b + 1)
                for t in range(NT):
                    last = tr(ps[:, 5, cols(t)], x2[:, t, :], ident[:])
                last.then_inc(pe_x2, 1)
                pe.wait_ge(act_x2T, 1 * b + 1)
                mm(ps[:, 6, :], wq1[:].rearrange("p a d -> p (a d)"), x2T[:], start=True, stop=True).then_inc(pe_x2, 1)
                mm(ps[:, 5, :], wk1[:].rearrange("p a d -> p (a d)"), x2T[:], start=True, stop=True).then_inc(pe_x2, 1)

            def project1_v(b):
                pe.wait_ge(dve_q1, 1 * b + 1)
                for t in range(NT):
                    last = mm(ps[:, 6, cols(t)], x2T[:, cols(t)], wv1[:], start=True, stop=True)
                last.then_inc(pe_x2, 1)

            def scores1(b, n):
                t0, nt = GROUPS1[n]
                if n == 0:
                    pe.wait_ge(dve_k1, 1 * b + 1)
                elif n == 1:
                    pe.wait_ge(act_qkv, 3 * b + 3)
                else:
                    pe.wait_ge(dve_r3, NB1 * b + 1)
                col = 0
                for t in range(t0, t0 + nt):
                    w = (t + 1) * P
                    dst = ps[:, 5 + n % 2, col:col + w]
                    mm(dst, q1[:, cols(t)], k1a[:, 0:w], start=True, stop=False)
                    mm(dst, q1[:, cols(t)], k1b[:, 0:w], start=False, stop=False)
                    last = mm(dst[:, t * P:w], ident_h[:], future_h[:, 0, :], start=False, stop=True)
                    col += w
                last.then_inc(pe_s1, 1)

            def transpose_p1(b, n):
                t0, nt = GROUPS1[n]
                pe.wait_ge(act_p1, NB1 * b + n + 1)
                for k in range(sum(t + 1 for t in range(t0, t0 + nt))):
                    last = tr(ps[:, 5 + n % 2, cols(k)], prob1[n][:, cols(k)], ident[:])
                last.then_inc(pe_pT, 1)

            def values1(b, n):
                t0, nt = GROUPS1[n]
                pe.wait_ge(dve_pT, NB1 * b + n + 1)
                k = 0
                for t in range(t0, t0 + nt):
                    for kb in range(t + 1):
                        last = mm(ps[:, 5 + n % 2, cols(t - t0)], probT1[n][:, cols(k)], v1[:, kb, :],
                                  start=(kb == 0), stop=(kb == t))
                        k += 1
                last.then_inc(pe_av1, 1)

            def transpose_x3(b):
                pe.wait_ge(dve_x3, 1 * b + 1)
                for t in range(NT):
                    last = tr(ps[:, 6, cols(t)], x3[:, t, :], ident[:])
                last.then_inc(pe_x3, 1)

            def hidden1(b, f):
                if f == 0:
                    pe.wait_ge(dve_x3lo, 1 * b + 1)
                if f >= 2:
                    pe.wait_ge(act_h1, NF * b + f - 1)
                split3(ps[:, 5 + f % 2, :], f1_hi[:, cols(f)], f1_lo[:, cols(f)],
                       x3_hi[:], x3_lo[:]).then_inc(pe_h1, 1)

            def output1(b):
                pe.wait_ge(act_h1, NF * (b + 1))
                pe.wait_ge(act_relu, NF * (b + 1))
                for t in range(NT):
                    for f in range(NF):
                        last = mm(ps[:, 5, cols(t)], actT[:, f, cols(t)], f2[:, f, :], start=(f == 0),
                                  stop=(f == NF - 1))
                last.then_inc(pe_y, 1)

            pe.wait_ge(w_pool, Z_CONST)
            pe.wait_ge(w_in, 16 * N_SMALL)
            tr(ps[:, 5, 0:N_VEC], vec_rows[:], ident[0:N_VEC, 0:N_VEC]).then_inc(w_pe, 1)
            project(0)
            project_qk(0)
            project_v(0)

            def element(b, more, back):
                prev = b - 1
                chunk = 0
                for j in range(NG):
                    scores_for_max(b, j)
                    while back and chunk < NT * E and (chunk + 1) * 42 <= (j + 1) * NT * E:
                        experts_down(prev, chunk // E, chunk % E)
                        chunk += 1
                transpose_max(b)
                if back:
                    project1(prev)
                    project1_v(prev)
                for n in range(NQ):
                    exact_unit(b, n)
                    if n % NU == 2 and n > NU:
                        values(b, n // NU - 1)
                    for step, at in zip((scores1, transpose_p1, values1), (S1, T1, V1)):
                        for k in range(NB1):
                            if back and at[k] == n:
                                step(prev, k)
                values(b, G - 1)
                for t in range(NT):
                    transpose_o(b, t)
                if back:
                    transpose_x3(prev)
                    hidden1(prev, 0)
                    hidden1(prev, 1)
                transpose_z(b)
                if back:
                    hidden1(prev, 2)
                project_out(b)
                if back:
                    hidden1(prev, 3)
                transpose_x1(b)
                if back:
                    output1(prev)
                if first(b):
                    pe.wait_ge(w_lo, 7)
                for m in range(NM):
                    experts_up(b, m)
                    if m == 1:
                        gate(b)
                    if more and m == 3:
                        project(b + 1)
                    if more and m == 5:
                        project_qk(b + 1)
                    if more and m == 8:
                        project_v(b + 1)
                if first(b):
                    pe.wait_ge(w_down_in, 16 * 2 * E)

            element(0, True, False)
            with pe.Fori(1, B - 1) as b:
                element(b, True, True)
            element(B - 1, False, True)
            for chunk in range(NT * E):
                experts_down(last_b, chunk // E, chunk % E)
            project1(last_b)
            project1_v(last_b)
            for k in (0, 2):
                for step in (scores1, transpose_p1, values1):
                    for n in range(k, min(k + 2, NB1)):
                        step(last_b, n)
            transpose_x3(last_b)
            for f in range(NF):
                hidden1(last_b, f)
            output1(last_b)

        @block.vector
        def _(dve):
            ve = nc.vector
            front = Chain(dve, ch0, N_FRONT)
            back = Chain(dve, ch1, N_BACK)

            def per_tile(ap):
                return ap.unsqueeze(2).to_broadcast([P, NT, D])

            def layer_norm(chain, n, src, dst, done):
                link, s = chain.link, ln_s[n]
                for t in range(NT):
                    last = ve.bn_stats(stats[n][:, t, :], src[:, t, :])
                link(last)
                ve.memset(s[:, 2, 0:1], 0.0)
                for t in range(NT):
                    last = ve.bn_aggr(mv[n][:, t, :], stats[n][:, t, :])
                link(last)
                link(ve.tensor_scalar(s[:, 0, :], mv[n][:, :, 1], EPS, None, ALU.add))
                link(ve.tensor_scalar(s[:, 1, :].bitcast(I32), s[:, 0, :].bitcast(I32), -0.5, RSQRT_SEED,
                                      ALU.mult, ALU.add))
                for _ in range(3):
                    link(ve.tensor_tensor(s[:, 2, :], s[:, 1, :], s[:, 1, :], ALU.mult))
                    link(ve.scalar_tensor_tensor(s[:, 3, :], s[:, 2, :], -0.5, s[:, 0, :], ALU.mult, ALU.mult))
                    link(ve.scalar_tensor_tensor(s[:, 1, :], s[:, 3, :], 1.5, s[:, 1, :], ALU.add, ALU.mult))
                for t in range(NT):
                    last = ve.tensor_scalar(dst[:, t, :], src[:, t, :], mv[n][:, t, 0:1], s[:, 1, t:t + 1],
                                            ALU.subtract, ALU.mult)
                last.then_inc(done, 1)

            def part(b, which, a):
                dst, src, bias, rows = ((qparts, ps[:, 7, :], bq_c, P),
                                        (kparts, ps[0:KV, 4, :], bk_c[0:KV], KV))[which]
                work = part_f[0:rows, :]
                if a == 0:
                    dve.wait_ge(pe_proj, 4 * b + 2 + which)
                    if which:
                        dve.wait_ge(dve_qk, 2 * b + 1)
                    elif not first(b):
                        dve.wait_ge(qk_out, 32 * b)
                    ve.tensor_scalar(work, src, bias, None, ALU.add).then_inc(dve_part, 1)
                    dve.wait_ge(dve_part, 3 * b + 1 + which)
                ins = ve.tensor_copy(dst[:, a, :], work)
                if a < PARTS - 1:
                    front.link(ins)
                    front.link(ve.tensor_tensor(work, work, dst[:, a, :], ALU.subtract))
                else:
                    ins.then_inc(dve_qk, 1)

            def values_in(b):
                dve.wait_ge(pe_proj, 4 * b + 4)
                if not first(b):
                    dve.wait_ge(pe_av, G * b)
                ve.tensor_tensor(vext[:, :, :, 0:HD],
                                 ps[:, 7, 0:NT * KV].rearrange("p (t h d) -> p t h d", t=NT, h=H),
                                 bv_r[:].rearrange("p (a h d) -> p a h d", a=1, h=H).to_broadcast([P, NT, H, HD]),
                                 ALU.add).then_inc(dve_part, 1)

            def maxima(b, j):
                qt, h0, hn = MAX_GROUPS[j]
                n = (qt + 1) * P
                dve.wait_ge(pe_max, NG * b + j + 1)
                if j == 0 and not first(b):
                    dve.wait_ge(pe_mrow, 1 * b)
                ve.tensor_reduce(negmax[:, qt, h0:h0 + hn],
                                 ps[:, MAX_BANKS[j % len(MAX_BANKS)], 0:hn * n].rearrange("p (h n) -> p h n", h=hn),
                                 axis=AX.X, op=ALU.max, negate=True).then_inc(dve_max, 1)

            def max_parts(b):
                dve.wait_ge(pe_mrow, 1 * b + 1)
                if not first(b):
                    dve.wait_ge(m_out, 16 * b)
                ve.tensor_copy(mrow[:], ps[0:NH, 4, :]).then_inc(dve_mrow, 1)
                dve.wait_ge(dve_mrow, 2 * b + 1)
                for a in range(PARTS):
                    ins = ve.tensor_copy(mparts[:, a, :], mrow[:])
                    if a < PARTS - 1:
                        front.link(ins)
                        front.link(ve.tensor_tensor(mrow[:], mrow[:], mparts[:, a, :], ALU.subtract))
                ins.then_inc(dve_mrow, 1)

            def divide(b, t):
                dve.wait_ge(pe_o, NT * b + t + 1)
                if t == 0 and not first(b):
                    dve.wait_ge(dve_z, 1 * b)
                heads = ps[:, (7, 4)[t % 2], :].rearrange("p (h c) -> p h c", c=32)
                front.link(ve.reciprocal(rden0[:, t, :], heads[:, :, HD]))
                ve.tensor_tensor(att[:, t, :].rearrange("p (h c) -> p h c", c=HD), heads[:, :, 0:HD],
                                 rden0[:, t, :].unsqueeze(2).to_broadcast([P, NH, HD]),
                                 ALU.mult).then_inc(dve_o, 1)

            def norm_z(b):
                dve.wait_ge(dve_o, NT * (b + 1))
                if not first(b):
                    dve.wait_ge(pe_tail, 4 * b)
                layer_norm(front, 0, att, attn, dve_z)

            def norm_x1(b):
                dve.wait_ge(pe_tail, 4 * b + 2)
                dve.wait_ge(x_res, 1 * b + 1)
                ve.tensor_tensor(res1[:].rearrange("p t d -> p (t d)"), ps[:, 4, :],
                                 xres[:].rearrange("p t d -> p (t d)"), ALU.add).then_inc(dve_wo, 1)
                dve.wait_ge(dve_wo, 1 * b + 1)
                if not first(b):
                    dve.wait_ge(dve_y2, NT * b)
                layer_norm(front, 0, res1, x1, dve_x1)

            def x1_lower(b):
                dve.wait_ge(act_x1T, 2 * b + 2)
                if not first(b):
                    dve.wait_ge(pe_up, 2 * NM * b)
                ve.tensor_tensor(x1_lo[:], x1T[:], x1_hi[:].bitcast(FP32), ALU.subtract).then_inc(dve_x1lo, 1)

            def gate_choice(b):
                dve.wait_ge(pe_tail, 4 * b + 4)
                ve.tensor_copy(lg[:].rearrange("p t e -> p (t e)"), ps[:, 4, 0:NT * E]).then_inc(dve_lg, 1)
                dve.wait_ge(dve_lg, 2 * b + 1)
                other = lg[:].unsqueeze(2).to_broadcast([P, NT, E, E])
                own = lg[:].unsqueeze(3).to_broadcast([P, NT, E, E])
                ve.tensor_tensor(cmp4[:, 0], other, own, ALU.is_gt)
                front.link(ve.tensor_tensor(cmp4[:, 1], other, own, ALU.is_equal))
                front.link(ve.tensor_tensor(cmp4[:, 1].rearrange("p t e j -> p t (e j)"),
                                            cmp4[:, 1].rearrange("p t e j -> p t (e j)"),
                                            before[:].rearrange("p e j -> p (e j)").unsqueeze(1)
                                            .to_broadcast([P, NT, E * E]), ALU.mult))
                front.link(ve.tensor_tensor(cmp4[:, 0], cmp4[:, 0], cmp4[:, 1], ALU.add))
                front.link(ve.tensor_reduce(lgx[:, 0], cmp4[:, 0], axis=AX.X, op=ALU.add))
                front.link(ve.tensor_scalar(lgx[:, 0], lgx[:, 0], 2.0, 0.5, ALU.is_lt, ALU.mult))
                front.link(ve.tensor_tensor(lgx[:, 1], lgx[:, 0], lg[:], ALU.mult))
                front.link(ve.tensor_reduce(lgs[:], lgx[:, 1], axis=AX.X, op=ALU.add))
                ve.tensor_tensor(lgx[:, 2], lg[:], lgs[:].unsqueeze(2).to_broadcast([P, NT, E]),
                                 ALU.subtract).then_inc(dve_lg, 1)

            def gate_weights(b):
                dve.wait_ge(act_gate, 1 * b + 1)
                ve.scalar_tensor_tensor(cw[:], lgx[:, 3], 1.0, lgx[:, 0], ALU.add, ALU.mult).then_inc(dve_cw, 1)

            def expert_hidden(b, m):
                dve.wait_ge(act_silu, NM * b + m + 1)
                dve.wait_ge(pe_up, 2 * NM * b + 2 * m + 2)
                if m == 0:
                    dve.wait_ge(pe_av, G * (b + 1))
                ve.tensor_tensor(hidT[:, m, :], silu[:, m % 2, :], ps[:, 2 * (m % 2) + 1, :],
                                 ALU.mult).then_inc(dve_hid, 1)

            def mix(b, t):
                if t == 0:
                    back.begin(b)
                    dve.wait_ge(dve_cw, 1 * b + 1)
                dve.wait_ge(pe_down, NT * b + t + 1)
                src = x1
                for e in range(E):
                    ins = ve.scalar_tensor_tensor(res[:, t, :], ps[:, 5 + t % 2, e * D:(e + 1) * D],
                                                  cw[:, t, e:e + 1], src[:, t, :], ALU.mult, ALU.add)
                    src = res
                    if e < E - 1:
                        back.link(ins)
                ins.then_inc(dve_y2, 1)

            def norm_x2(b):
                dve.wait_ge(dve_y2, NT * (b + 1))
                layer_norm(back, 1, res, x2, dve_x2)

            def qk_halves1(b):
                dve.wait_ge(act_qkv, 3 * b + 1)
                ve.tensor_tensor(q1[64:P, :], ps[64:P, 6, :], q1[64:P, :].bitcast(FP32),
                                 ALU.subtract).then_inc(dve_q1, 1)
                dve.wait_ge(act_qkv, 3 * b + 2)
                ve.tensor_copy(k1b[64:P, :], ps[64:P, 5, :])
                back.link(ve.tensor_tensor(k1b[0:64, :], ps[0:64, 5, :], k1a[0:64, :].bitcast(FP32),
                                           ALU.subtract))
                ve.tensor_tensor(k1a[64:P, :], ps[64:P, 5, :], k1a[64:P, :].bitcast(FP32),
                                 ALU.subtract).then_inc(dve_k1, 1)

            def maximum1(b, n):
                t0, nt = GROUPS1[n]
                dve.wait_ge(pe_s1, NB1 * b + n + 1)
                col = 0
                for t in range(t0, t0 + nt):
                    w = (t + 1) * P
                    last = ve.tensor_reduce(nmax1[:, 0, t:t + 1], ps[:, 5 + n % 2, col:col + w], axis=AX.X,
                                            op=ALU.max, negate=True)
                    col += w
                back.link(last)
                ve.tensor_scalar(nmax1[:, 1, t0:t0 + nt], nmax1[:, 0, t0:t0 + nt], SCALE1, None,
                                 ALU.mult).then_inc(dve_m1, 1)

            def probs_out1(b, n):
                t0, nt = GROUPS1[n]
                dve.wait_ge(pe_pT, NB1 * b + n + 1)
                if n == 2:
                    dve.wait_ge(pe_av1, NB1 * b + 1)
                w = P * sum(t + 1 for t in range(t0, t0 + nt))
                ve.tensor_copy(probT1[n][:, 0:w], ps[:, 5 + n % 2, 0:w]).then_inc(dve_pT, 1)

            def attend1(b, n):
                t0, nt = GROUPS1[n]
                dve.wait_ge(act_p1, NB1 * b + n + 1)
                back.link(ve.reciprocal(den1[:, 1, t0:t0 + nt], den1[:, 0, t0:t0 + nt]))
                dve.wait_ge(pe_av1, NB1 * b + n + 1)
                for t in range(t0, t0 + nt):
                    last = ve.scalar_tensor_tensor(res[:, t, :], ps[:, 5 + n % 2, (t - t0) * D:(t - t0 + 1) * D],
                                                   den1[:, 1, t:t + 1], x2[:, t, :], ALU.mult, ALU.add)
                last.then_inc(dve_r3, 1)

            def norm_x3(b):
                dve.wait_ge(dve_r3, NB1 * (b + 1))
                layer_norm(back, 1, res, x3, dve_x3)

            def x3_lower(b):
                dve.wait_ge(act_x3, 1 * b + 1)
                ve.tensor_tensor(x3_lo[:], ps[:, 6, :], x3_hi[:].bitcast(FP32), ALU.subtract).then_inc(dve_x3lo, 1)

            def angle(b, f):
                dve.wait_ge(act_h1, NF * b + f + 1)
                if f:
                    dve.wait_ge(dve_ang, NF * b + f)
                a = ang[:, f % 2, :]
                back.link(ve.tensor_scalar(ang_n[:], a, ROUND, ROUND, ALU.add, ALU.subtract))
                ve.tensor_tensor(a, a, ang_n[:], ALU.subtract).then_inc(dve_ang, 1)

            def activate(b, f):
                dve.wait_ge(act_sin, NF * b + f + 1)
                ve.scalar_tensor_tensor(actT[:, f, :], ang[:, f % 2, :], th[:, 1, f:f + 1],
                                        hid1[:, f % 2, :], ALU.mult, ALU.add).then_inc(dve_act, 1)

            def norm_out(b):
                dve.wait_ge(pe_y, 1 * b + 1)
                dve.wait_ge(pool_x3, 1 * b + 1)
                back.link(ve.tensor_tensor(res[:].rearrange("p t d -> p (t d)"), ps[:, 5, :],
                                           x3[:].rearrange("p t d -> p (t d)"), ALU.add))
                dve.wait_ge(y_out, 16 * b + 1)
                layer_norm(back, 1, res, y, dve_y)
                back.end()

            def prepare():
                k = [1]

                def step(ins):
                    k[0] += 1
                    ins.then_inc(w_dve, 1)
                    dve.wait_ge(w_dve, k[0])

                step(ve.tensor_scalar(th[:, 6, :], theta_c, 1.0 / TWO_PI, None, ALU.mult))
                step(ve.tensor_scalar(th[:, 6, :], th[:, 6, :], ROUND, ROUND, ALU.add, ALU.subtract))
                step(ve.scalar_tensor_tensor(th[:, 7, :], th[:, 6, :], -PI_C1, theta_c, ALU.mult, ALU.add))
                step(ve.scalar_tensor_tensor(th[:, 7, :], th[:, 6, :], -PI_C2, th[:, 7, :], ALU.mult, ALU.add))
                step(ve.tensor_scalar(th[:, 7, :], th[:, 7, :], 1.0 / TWO_PI, 0.5, ALU.mult, ALU.min))
                step(ve.tensor_scalar(th[:, 2, :], th[:, 7, :], -0.5, None, ALU.max))
                step(ve.tensor_scalar(th[:, 7, :], th[:, 2, :], 0.25, None, ALU.add))
                step(ve.tensor_scalar(th[:, 6, :], th[:, 7, :], ROUND, ROUND, ALU.add, ALU.subtract))
                step(ve.tensor_tensor(th[:, 3, :], th[:, 7, :], th[:, 6, :], ALU.subtract))
                assert k[0] == W_TURNS
                dve.wait_ge(w_act, 1)
                step(ve.tensor_tensor(th[:, 6, :], th[:, 5, :], w_real_c, ALU.mult))
                step(ve.tensor_tensor(th[:, 7, :], th[:, 4, :], w_imag_c, ALU.mult))
                step(ve.tensor_tensor(th[:, 6, :], th[:, 6, :], th[:, 7, :], ALU.add))
                step(ve.scalar_tensor_tensor(th[:, 0, :], fb1_c, 0.1 / TWO_PI, th[:, 2, :], ALU.mult, ALU.add))
                step(ve.scalar_tensor_tensor(th[:, 1, :], th[:, 6, :], 0.1, w_imag_c, ALU.mult, ALU.mult))

            ve.memset(qstack[64:P].rearrange("p h n -> p (h n)").bitcast(FP32), 0.0)
            ve.memset(kstack[64:P].rearrange("p h n -> p (h n)").bitcast(FP32), 0.0).then_inc(w_zero, 1)
            dve.wait_ge(w_zero, 1)
            ve.memset(kstack[ROWS:ROWS + PARTS], 1.0).then_inc(w_zero, 1)
            dve.wait_ge(w_in, 16 * N_SMALL)
            dve.wait_ge(w_pe, 1)
            ve.tensor_copy(vecs[:], ps[:, 5, 0:N_VEC]).then_inc(w_dve, 1)
            dve.wait_ge(w_dve, 1)
            front.begin(0)
            for which in range(2):
                for a in range(PARTS):
                    part(0, which, a)
            values_in(0)
            front.pause()

            def element(b, more, has_back):
                prev = b - 1
                front.begin(b, N_PARTS)
                t = 0
                for j in range(NG):
                    maxima(b, j)
                    while has_back and t < NT - 1 and (t + 1) * 11 + 3 <= j:
                        mix(prev, t)
                        t += 1
                if has_back:
                    mix(prev, NT - 1)
                max_parts(b)
                if first(b):
                    prepare()
                if has_back:
                    norm_x2(prev)
                    qk_halves1(prev)
                    for k in (0, 2):
                        for step in (maximum1, probs_out1, attend1):
                            for n in range(k, min(k + 2, NB1)):
                                step(prev, n)
                    norm_x3(prev)
                for t in range(NT):
                    divide(b, t)
                if has_back:
                    x3_lower(prev)
                norm_z(b)
                if has_back:
                    angle(prev, 0)
                    angle(prev, 1)
                    activate(prev, 0)
                    activate(prev, 1)
                norm_x1(b)
                if has_back:
                    angle(prev, 2)
                    angle(prev, 3)
                x1_lower(b)
                if has_back:
                    activate(prev, 2)
                    activate(prev, 3)
                gaps = [(part, which, a) for which in range(2) for a in range(PARTS)]
                for m in range(NM):
                    expert_hidden(b, m)
                    if m == 2:
                        gate_choice(b)
                    if m == 4:
                        gate_weights(b)
                        front.end()
                        if more:
                            front.begin(b + 1)
                    if more and 6 <= m < 6 + len(gaps):
                        part(b + 1, *gaps[m - 6][1:])
                    if more and m == 6 + len(gaps):
                        values_in(b + 1)
                        front.pause()
                    if has_back and m == 15:
                        norm_out(prev)

            element(0, True, False)
            with dve.Fori(1, B - 1) as b:
                element(b, True, True)
            element(B - 1, False, True)
            last_b = B - 1
            for t in range(NT):
                mix(last_b, t)
            norm_x2(last_b)
            qk_halves1(last_b)
            for k in (0, 2):
                for step in (maximum1, probs_out1, attend1):
                    for n in range(k, min(k + 2, NB1)):
                        step(last_b, n)
            norm_x3(last_b)
            x3_lower(last_b)
            angle(last_b, 0)
            angle(last_b, 1)
            activate(last_b, 0)
            activate(last_b, 1)
            angle(last_b, 2)
            angle(last_b, 3)
            activate(last_b, 2)
            activate(last_b, 3)
            norm_out(last_b)


_INS = ['L0_attn_x', 'L0_attn_Wq', 'L0_attn_bq', 'L0_attn_Wk', 'L0_attn_bk', 'L0_attn_Wv', 'L0_attn_bv',
        'L0_attn_ln_g', 'L0_attn_ln_b', 'L0_attn_Wo', 'L0_attn_bo', 'L0_ffn_gate_w', 'L0_ffn_w1', 'L0_ffn_w2',
        'L0_ffn_w3', 'L1_attn_Wq', 'L1_attn_Wk', 'L1_attn_Wv', 'L1_ffn_W1', 'L1_ffn_b1',
        'L1_ffn_quantum_phases', 'L1_ffn_quantum_weights_real', 'L1_ffn_quantum_weights_imag', 'L1_ffn_W2',
        'L1_ffn_b2']


def kernel(**inputs):
    import concourse.bacc as _bacc
    from concourse.bass_utils import run_bass_kernel_spmd as _run

    nc = _bacc.Bacc("TRN2", target_bir_lowering=False, num_devices=1)
    arrays, args = {}, []
    for name in _INS:
        a = np.ascontiguousarray(inputs[name])
        arrays[f"in_{name}"] = a
        args.append(nc.dram_tensor(f"in_{name}", a.shape, mybir.dt.from_np(a.dtype), kind="ExternalInput").ap())
    args.append(nc.dram_tensor("out_0", (B, S, D), FP32, kind="ExternalOutput").ap())
    build(nc, *args)
    r = _run(nc, [arrays], core_ids=[0])
    return r.results[0]["out_0"]
```

```python
from contextlib import ExitStack

import numpy as np

import concourse.bass as bass
from concourse import mybir

FP32 = mybir.dt.float32
FP32R = mybir.dt.float32r
BF16 = mybir.dt.bfloat16
I32 = mybir.dt.int32
ALU = mybir.AluOpType
ACT = mybir.ActivationFunctionType
AX = mybir.AxisListType

P = 128
B, S, D = 4, 512, 128
NT = S // P
H, G, HD = 4, 4, 8
NH = H * G
KV = H * HD
PARTS = 3
TERMS = PARTS * PARTS
ROWS = 96
E, FF0 = 4, 704
FULL = FF0 // P
TAIL = FF0 - FULL * P
NM = E * FF0 // P
DQ = 64
FF1 = 512
NF = FF1 // P
EPS = 1e-5
NEG = -1e30
SCALE0 = float(HD) ** -0.5
SCALE1 = float(DQ) ** -0.5
TWO_PI = 2.0 * np.pi
PI_C1 = 6.28125
PI_C2 = float(np.float32(TWO_PI - PI_C1))
TURN = float(np.nextafter(np.float32(TWO_PI), np.float32(0)))
ROUND = 1.5 * 2.0 ** 23
RSQRT_SEED = float(0x5F3759DF)

MAX_GROUPS = [(qt, h0, hn) for qt, hn in ((0, 4), (1, 2), (2, 1), (3, 1)) for h0 in range(0, NH, 2 * hn)]
UNITS = [[(0, h, 0, 0), (3, h, 512, 384), (1, h, 640, 128)] for h in range(H)]
UNITS.append([(2, h, 256 * h, 256) for h in range(H)])
NU = len(UNITS)
PLACE = {(kb, h): (u, col, q0) for u, unit in enumerate(UNITS) for kb, h, col, q0 in unit}
DOWN_BANKS = (5, 6, 7, 4)
W1_BANKS = [(0, 2, 7, 4)[m % 4] for m in range(NM)]
W3_BANKS = [(1, 3)[m % 2] if m < 4 else (3, 6, 1)[m % 3] for m in range(NM)]
W1_BEFORE = [max([k for k in range(m) if W1_BANKS[k] == W1_BANKS[m]], default=None) for m in range(NM)]
W3_BEFORE = [max([k for k in range(m) if W3_BANKS[k] == W3_BANKS[m]], default=None) for m in range(NM)]
GROUPS1 = [(0, 2), (2, 1), (3, 1)]
NB1 = len(GROUPS1)
EXPERT_TILES = [[FULL * e + j for j in range(FULL)] + [E * FULL + e // 2] for e in range(E)]

W_TURNS = 10
N_FRONT = 35
N_BACK = 51
X1, S1, T1, V1, A1 = (6, 8, 10), (11, 12, 17), (14, 15, 19), (15, 16), (12, 13, 18)
FILL = (8, 3, 0, 3, 14)
TAIL_FILL = (16, 3, 3, 2, 4, 4, 14, 6, 8)
DOWN_PIECES = NT * E * 2
DOWN_EARLY = 21
LN_STAGES = 12
X3_EARLY = 3
OUT_AT = 14
SIN_AT = 3
N_VEC = 4 * NF + E + 4


def tiles_of(dst, src):
    pairs = [(dst[:, 0:E * FULL, :].rearrange("p (e n) c -> p e (n c)", e=E), src[:, :, 0:FULL * P])]
    for m in range(E // 2):
        pairs.append((dst[:, E * FULL + m, :].rearrange("p (e c) -> p e c", e=2),
                      src[:, 2 * m:2 * m + 2, FULL * P:FF0]))
    return pairs


class Chain:

    def __init__(self, eng, sem, per):
        self.eng, self.sem, self.per = eng, sem, per

    def begin(self, b):
        self.base, self.n = b * self.per, 0

    def mark(self, ins):
        self.n += 1
        ins.then_inc(self.sem, 1)

    def wait(self):
        self.eng.wait_ge(self.sem, self.base + self.n)

    def link(self, ins):
        self.mark(ins)
        self.wait()

    def end(self):
        assert self.n == self.per, (self.n, self.per)


def build(nc, x, Wq0, bq0, Wk0, bk0, Wv0, bv0, ln_g, ln_b, Wo0, bo0, gate_w, w1, w2, w3,
          Wq1, Wk1, Wv1, fW1, fb1, theta, w_real, w_imag, fW2, fb2, out):
    ctx = ExitStack()
    with ctx:
        def sb(name, shape, dt=FP32):
            return ctx.enter_context(nc.sbuf_tensor(name, shape, dt))

        def sem(name):
            return ctx.enter_context(nc.semaphore(name))

        ident = sb("ident", [P, P])
        ident_h = sb("ident_h", [P, P], BF16)
        future_h = sb("future_h", [P, 4, P], BF16)
        before = sb("before", [P, E, E])
        wq0 = sb("wq0", [P, D])
        wk0 = sb("wk0", [P, KV])
        wv0 = sb("wv0", [P, KV])
        wo0 = sb("wo0", [P, D])
        vec_rows = sb("vec_rows", [N_VEC, P])
        vecs = sb("vecs", [P, N_VEC])
        theta_c, w_real_c, w_imag_c, fb1_c = (vecs[:, NF * n:NF * (n + 1)] for n in range(4))
        gateT = vecs[:, 4 * NF:4 * NF + E]
        bq_c, lng_c, lnb_c, bk_c = (vecs[:, 4 * NF + E + n:4 * NF + E + n + 1] for n in range(4))
        bv_r = sb("bv_r", [P, KV])
        bo_r = sb("bo_r", [P, D])
        b2_r = sb("b2_r", [P, D])
        up_hi = [sb(f"up{n}_hi", [P, NM, P], FP32R) for n in range(2)]
        up_lo = [sb(f"up{n}_lo", [P, NM, P], FP32R) for n in range(2)]
        down = sb("down", [P, E * (FULL + 1), D])
        wq1 = sb("wq1", [P, 2, DQ])
        wk1 = sb("wk1", [P, 2, DQ])
        wv1 = sb("wv1", [P, D])
        f1 = sb("f1", [P, FF1])
        f1_hi = sb("f1_hi", [P, FF1], FP32R)
        f1_lo = sb("f1_lo", [P, FF1], FP32R)
        f2 = sb("f2", [P, NF, D])
        th = sb("th", [P, 8, NF])
        xin = sb("xin", [P, NT, D])
        xres = sb("xres", [P, NT, D])
        zT = sb("zT", [P, S])
        qparts = sb("qparts", [P, PARTS, S], BF16)
        kparts = sb("kparts", [KV, PARTS, S], BF16)
        qstack = sb("qstack", [P, NH, S], BF16)
        kstack = sb("kstack", [P, H, S], BF16)
        vext = sb("vext", [P, NT, H, 32])
        negmax = sb("negmax", [P, NT, NH])
        mrow = sb("mrow", [NH, S])
        mparts = sb("mparts", [NH, PARTS, S], BF16)
        hidT = sb("hidT", [P, NM, S])
        flat = hidT[:].rearrange("p a b -> p (a b)")
        probs = flat[:, 0:2 * NU * 1024].rearrange("p (a u n) -> p a u n", a=2, u=NU)
        stage = flat[:, 0:2 * E * FF0].rearrange("p (w e n) -> p w e n", w=2, e=E)
        uT = sb("uT", [P, G, S])
        rden0 = sb("rden0", [P, NT, NH])
        att = sb("att", [P, NT, D])
        attn = sb("attn", [P, NT, D])
        res1 = att
        x1 = sb("x1", [P, NT, D])
        x1T = sb("x1T", [P, S])
        x1_hi = sb("x1_hi", [P, S], FP32R)
        x1_lo = sb("x1_lo", [P, S], FP32R)
        lg = sb("lg", [P, NT, E])
        lgx = sb("lgx", [P, 4, NT, E])
        cmp4 = sb("cmp4", [P, 2, NT, E, E])
        lgs = sb("lgs", [P, NT])
        cw = sb("cw", [P, NT, E])
        silu = sb("silu", [P, 3, S])
        rest = (silu[:, 1, :], silu[0:KV, 2, :])
        spare = sb("spare", [P, 3])
        res = sb("res", [P, NT, D])
        x2 = sb("x2", [P, NT, D])
        four = sb("four", [P, 4, S])
        x2T = four[:, 0, :]
        v1 = four[:, 1, :].rearrange("p (t d) -> p t d", t=NT)
        ang = four
        ang_n = sb("ang_n", [P, S])
        prob1 = (four[:, 2, :], ang_n[:], four[:, 2, :])
        probT1 = (four[:, 3, :], four[:, 0, :], four[:, 3, :])
        q1 = sb("q1", [P, S], FP32R)
        k1a = sb("k1a", [P, S], FP32R)
        k1b = sb("k1b", [P, S], FP32R)
        x3_hi, x3_lo = q1, k1a
        nmax1 = sb("nmax1", [P, 2, NT])
        den1 = sb("den1", [P, 2, NT])
        x3 = sb("x3", [P, NT, D])
        actT = uT
        y = sb("y", [P, NT, D])
        xT = y[:].rearrange("p t d -> p (t d)")
        carry = sb("carry", [P, 1 + G * NU])
        stats = [sb(f"stats{n}", [P, NT, 6]) for n in range(2)]
        mv = [sb(f"mv{n}", [P, NT, 2]) for n in range(2)]
        ln_s = [sb(f"ln_s{n}", [P, 4, NT]) for n in range(2)]

        ps = ctx.enter_context(nc.psum_tensor("ps", [P, 8, 512], FP32))
        q_scr = nc.dram_tensor("q_scr", (PARTS, HD, NH, S), BF16, kind="Internal").ap()
        k_scr = nc.dram_tensor("k_scr", (PARTS, HD, H, S), BF16, kind="Internal").ap()

        w_first = sem("w_first")
        w_in = sem("w_in")
        w_up_in = sem("w_up_in")
        w_down_in = sem("w_down_in")
        w_pool = sem("w_pool")
        w_zero = sem("w_zero")
        w_dve = sem("w_dve")
        w_act = sem("w_act")
        w_hi = sem("w_hi")
        w_lo = sem("w_lo")
        w_pe = sem("w_pe")
        x_in = sem("x_in")
        x_res = sem("x_res")
        qk_out = sem("qk_out")
        qk_in = sem("qk_in")
        m_in = sem("m_in")
        y_out = sem("y_out")
        pe_proj = sem("pe_proj")
        pe_max = sem("pe_max")
        pe_mrow = sem("pe_mrow")
        pe_unit = sem("pe_unit")
        pe_av = sem("pe_av")
        pe_o = sem("pe_o")
        pe_tail = sem("pe_tail")
        pe_up = sem("pe_up")
        act_xT = sem("act_xT")
        act_exp = sem("act_exp")
        act_zT = sem("act_zT")
        act_x1T = sem("act_x1T")
        act_gate = sem("act_gate")
        act_silu = sem("act_silu")
        pool_mask = sem("pool_mask")
        dve_part = sem("dve_part")
        act_part = sem("act_part")
        dve_qk = sem("dve_qk")
        dve_max = sem("dve_max")
        dve_mrow = sem("dve_mrow")
        dve_uT = sem("dve_uT")
        dve_o = sem("dve_o")
        dve_z = sem("dve_z")
        dve_wo = sem("dve_wo")
        dve_x1 = sem("dve_x1")
        dve_x1lo = sem("dve_x1lo")
        dve_lg = sem("dve_lg")
        dve_cw = sem("dve_cw")
        dve_hid = sem("dve_hid")
        ch0 = sem("ch0")
        pe_down = sem("pe_down")
        pe_x2 = sem("pe_x2")
        pe_s1 = sem("pe_s1")
        pe_pT = sem("pe_pT")
        pe_av1 = sem("pe_av1")
        pe_x3 = sem("pe_x3")
        pe_h1 = sem("pe_h1")
        pe_y = sem("pe_y")
        act_qk1 = sem("act_qk1")
        act_p1 = sem("act_p1")
        act_x3 = sem("act_x3")
        act_h1 = sem("act_h1")
        act_sin = sem("act_sin")
        act_relu = sem("act_relu")
        pool_x3 = sem("pool_x3")
        dve_y2 = sem("dve_y2")
        dve_x2 = sem("dve_x2")
        dve_x2T = sem("dve_x2T")
        dve_v1 = sem("dve_v1")
        dve_q1 = sem("dve_q1")
        dve_k1 = sem("dve_k1")
        dve_m1 = sem("dve_m1")
        dve_pT = sem("dve_pT")
        dve_r3 = sem("dve_r3")
        dve_x3 = sem("dve_x3")
        dve_x3lo = sem("dve_x3lo")
        dve_ang = sem("dve_ang")
        dve_act = sem("dve_act")
        dve_y = sem("dve_y")
        ch1 = sem("ch1")
        NG = len(MAX_GROUPS)
        NQ = G * NU

        block = ctx.enter_context(nc.Block())

        x_v = x.rearrange("b (t p) d -> b p t d", p=P)
        out_v = out.rearrange("b (t p) d -> b p t d", p=P)

        def row(ap, n):
            return ap.rearrange("(a n) -> a n", a=1).to_broadcast([P, n])


        N_FIRST, N_SMALL = 13, 10
        Z_DOWN, Z_CONST = 2, 8

        def final(b):
            return isinstance(b, int) and b == B - 1

        def bank1(b, n):
            return (5, 6, 0 if final(b) else 5)[n]

        def first(b):
            return isinstance(b, int) and b == 0

        @block.sync
        def _(sp):
            def load(dst, src, done=w_in):
                sp.dma_start(dst, src).then_inc(done, 16)

            def load_x(b):
                if not first(b):
                    sp.wait_ge(x_res, 1 * b)
                sp.dma_start(xin[:], x_v[bass.ds(b, 1)].rearrange("a p t d -> p (a t) d")).then_inc(x_in, 16)

            def restack(b):
                for n, (scr, parts) in enumerate(((q_scr, qparts), (k_scr, kparts))):
                    sp.wait_ge(dve_qk, 2 * b + 1 + n)
                    for a in range(PARTS):
                        sp.dma_start(scr[a].rearrange("d h n -> h d n"), parts[:, a, :]).then_inc(qk_out, 16)
                sp.wait_ge(qk_out, 16 * 2 * PARTS * (b + 1))
                for a in range(PARTS):
                    rows = slice(PARTS * HD * a, PARTS * HD * (a + 1))
                    sp.dma_start(qstack[rows], q_scr[a].rearrange("d h n -> d (h n)").unsqueeze(0)
                                 .to_broadcast([PARTS, HD, NH * S])).then_inc(qk_in, 16)
                sp.dma_start(kstack[0:TERMS * HD], k_scr.rearrange("c d h n -> (c d) (h n)").unsqueeze(0)
                             .to_broadcast([PARTS, PARTS * HD, H * S])).then_inc(qk_in, 16)

            def restack_max(b):
                sp.wait_ge(dve_mrow, 2 * b + 2)
                for a in range(PARTS):
                    sp.dma_start(qstack[ROWS + a:ROWS + a + 1], mparts[:, a, :]).then_inc(m_in, 16)

            def store(b):
                sp.wait_ge(dve_y, 1 * b + 1)
                sp.dma_start(out_v[bass.ds(b, 1)].rearrange("a p t d -> p (a t) d"), y[:]).then_inc(y_out, 16)

            load_x(0)
            sp.wait_ge(w_pool, 1)
            for n, v in enumerate((theta, w_real, w_imag, fb1)):
                load(vec_rows[NF * n:NF * (n + 1), :], v.rearrange("(f p) -> f p", p=P), w_first)
            load(vec_rows[4 * NF:4 * NF + E, :], gate_w[0:E, :], w_first)
            for n, v in enumerate((bq0, ln_g, ln_b, bk0)):
                k = 4 * NF + E + n
                load(vec_rows[k:k + 1, 0:v.shape[0]], v.rearrange("(a n) -> a n", a=1), w_first)
            load(wq0[:], Wq0, w_first)
            load(wk0[:], Wk0, w_first)
            load(wv0[:], Wv0, w_first)
            load(bv_r[:], row(bv0, KV), w_first)
            load(bo_r[:], row(bo0, D))
            load(wo0[:], Wo0)
            load(f1[:], fW1)
            load(b2_r[:], row(fb2, D))
            load(wv1[:], Wv1)
            for half in range(2):
                load(wq1[:, half, :], Wq1)
                load(wk1[:, half, :], Wk1)
            load(f2[:], fW2.rearrange("(f p) d -> p f d", p=P))
            sp.wait_ge(w_zero, 2)
            restack(0)
            for w, src in enumerate((w1, w3)):
                sp.dma_start(stage[:, w], src[0:E].rearrange("e d n -> d e n")).then_inc(w_up_in, 16)
            sp.wait_ge(w_pool, Z_DOWN)
            for e in range(E):
                n0 = e * (FULL + 1)
                sp.dma_start(down[:, n0:n0 + FULL, :],
                             w2[e, 0:FULL * P, :].rearrange("(j p) d -> p j d", p=P)).then_inc(w_down_in, 16)
                p0 = TAIL * (e % 2)
                sp.dma_start(down[p0:p0 + TAIL, n0 + FULL, :], w2[e, FULL * P:, :]).then_inc(w_down_in, 16)
            def element(b, more):
                if more:
                    load_x(b + 1)
                restack_max(b)
                if more:
                    restack(b + 1)

            element(0, True)
            with sp.Fori(1, B - 1) as b:
                element(b, True)
                store(b - 1)
            element(B - 1, False)
            store(B - 2)
            store(B - 1)
            sp.wait_ge(y_out, 16 * B + 1)

        @block.gpsimd
        def _(pool):
            gp = nc.gpsimd
            gp.memset(vec_rows[:], 0.0).then_inc(w_pool, 1)
            gp.memset(down[:, FULL::FULL + 1, :], 0.0).then_inc(w_pool, 1)
            pool.wait_ge(w_pool, 1)
            gp.memset(ident[:], 0.0)
            gp.memset(future_h[:], 0.0)
            gp.memset(before[:], 1.0)
            gp.memset(carry[:], 0.0)
            gp.memset(vext[:], 0.0).then_inc(w_pool, 1)
            pool.wait_ge(w_pool, 3)
            gp.affine_select(out=ident[:], in_=ident[:], compare_op=ALU.not_equal, fill=1.0, base=0,
                             pattern=[[-1, P]], channel_multiplier=1).then_inc(w_pool, 1)
            gp.affine_select(out=future_h[:], in_=future_h[:], compare_op=ALU.is_ge, fill=NEG, base=0,
                             pattern=[[0, 4], [-1, P]], channel_multiplier=1).then_inc(w_pool, 1)
            gp.affine_select(out=before[:], in_=before[:], compare_op=ALU.is_gt, fill=0.0, base=0,
                             pattern=[[1, E], [-1, E]], channel_multiplier=0).then_inc(w_pool, 1)
            gp.memset(vext[:, :, :, HD:HD + 1], 1.0).then_inc(w_pool, 1)
            pool.wait_ge(w_pool, 4)
            gp.tensor_copy(ident_h[:], ident[:]).then_inc(w_pool, 1)
            gp.memset(spare[:, 2:3], 0.0).then_inc(y_out, 1)

            def residual_x(b):
                if first(b):
                    pool.wait_ge(pe_proj, 1)
                else:
                    pool.wait_ge(dve_wo, 1 * b)
                gp.tensor_tensor(xres[:], xin[:], bo_r[:].unsqueeze(1).to_broadcast([P, NT, D]),
                                 ALU.add).then_inc(x_res, 1)

            def masks(b):
                for g in range(G):
                    for u in range(NU):
                        n = NU * g + u
                        pool.wait_ge(act_exp, NQ * b + n + 1)
                        gp.tensor_tensor(carry[:, n + 1:n + 2], carry[:, 0:1], carry[:, 0:1], ALU.add)
                        pr = probs[:, g % 2, u, :]
                        if u < H:
                            spots = [(pr[:, 0:P], [[1, P]]),
                                     (pr[:, 512:512 + 2 * P].rearrange("p (a q) -> p a q", a=2), [[0, 2], [1, P]])]
                        else:
                            spots = [(pr.rearrange("p (a q) -> p a q", a=H)[:, :, 0:P], [[0, H], [1, P]])]
                        for spot, pattern in spots:
                            last = gp.affine_select(out=spot, in_=spot, compare_op=ALU.is_ge, fill=0.0, base=0,
                                                    pattern=pattern, channel_multiplier=-1)
                        last.then_inc(pool_mask, 1)

            def residual_x3(b):
                pool.wait_ge(pe_x3, 1 * b + 1)
                gp.tensor_tensor(x3[:], x3[:], b2_r[:].unsqueeze(1).to_broadcast([P, NT, D]),
                                 ALU.add).then_inc(pool_x3, 1)

            pool.wait_ge(w_pool, Z_CONST)
            pool.wait_ge(y_out, 1)
            pool.wait_ge(w_zero, 1)
            gp.memset(kstack[ROWS:ROWS + PARTS], 1.0).then_inc(w_zero, 1)
            pool.wait_ge(w_zero, 2)
            pool.wait_ge(w_in, 16 * N_SMALL)
            residual_x(0)
            for n, (hi, lo) in enumerate(zip(up_hi, up_lo)):
                for k, (dst, src) in enumerate(tiles_of(lo, stage[:, n])):
                    pool.wait_ge(w_hi, 3 * n + k + 1)
                    gp.tensor_tensor(dst, src, tiles_of(hi, stage[:, n])[k][0].bitcast(FP32),
                                     ALU.subtract).then_inc(w_lo, 1)
            pool.wait_ge(w_hi, 7)
            gp.tensor_tensor(f1_lo[:], f1[:], f1_hi[:].bitcast(FP32), ALU.subtract).then_inc(w_lo, 1)
            masks(0)
            residual_x(1)
            with pool.Fori(1, B - 1) as b:
                masks(b)
                residual_x3(b - 1)
                residual_x(b + 1)
            masks(B - 1)
            residual_x3(B - 2)
            residual_x3(B - 1)

        @block.scalar
        def _(act):
            sc = nc.scalar

            def xT_out(b):
                act.wait_ge(pe_proj, 4 * b + 1)
                if not (isinstance(b, int) and b < 3):
                    act.wait_ge(y_out, 16 * (b - 2) + 1)
                sc.activation(xT, ps[:, 0, :], ACT.Copy).then_inc(act_xT, 1)

            def load_table(func, n):
                sc.activation(spare[:, n:n + 1], ident[:, 0:1], func)

            def part(b, which, a):
                dst, src, bias = ((qparts, ps[:, 1, :], bq_c), (kparts, ps[0:KV, 2, :], bk_c[0:KV]))[which]
                if a == 0:
                    act.wait_ge(pe_proj, 4 * b + 2 + which)
                    if which == 0 and not first(b):
                        act.wait_ge(qk_out, 16 * 2 * PARTS * b)
                    sc.activation(dst[:, a, :], src, ACT.Identity, bias=bias).then_inc(act_part, 1)
                else:
                    act.wait_ge(dve_part, 3 * b + 1 + which)
                    sc.activation(dst[:, a, :], rest[which], ACT.Copy).then_inc(act_part, 1)

            def exps(b, n):
                g, u = n // NU, n % NU
                act.wait_ge(pe_unit, NQ * b + n + 1)
                if n == 0 and first(b):
                    act.wait_ge(w_lo, 7)
                if g < 2:
                    if u == 0 and not first(b):
                        act.wait_ge(pe_down, NT * b)
                else:
                    act.wait_ge(pe_av, G * b + g - 1)
                pair = 2 * (n % 2)
                sc.activation(probs[:, g % 2, u, :].rearrange("p (a n) -> p a n", a=2),
                              ps[:, pair:pair + 2, :], ACT.Exp, scale=SCALE0).then_inc(act_exp, 1)

            def zT_out(b):
                act.wait_ge(pe_tail, 4 * b + 1)
                sc.activation(zT[:], ps[:, 7, :], ACT.Identity, bias=lnb_c,
                              scale=lng_c).then_inc(act_zT, 1)

            def x1_hi_out(b):
                act.wait_ge(pe_tail, 4 * b + 3)
                if not first(b):
                    act.wait_ge(pe_up, 2 * NM * b)
                sc.activation(x1_hi[:], ps[:, 7, :], ACT.Copy).then_inc(act_x1T, 1)

            def x1T_out(b):
                act.wait_ge(dve_x1lo, 1 * b + 1)
                sc.activation(x1T[:], ps[:, 7, :], ACT.Copy).then_inc(act_x1T, 1)

            def gate_tanh(b):
                act.wait_ge(dve_lg, 2 * b + 2)
                sc.activation(lgx[:, 3], lgx[:, 2], ACT.Tanh).then_inc(act_gate, 1)

            def silus(b, m):
                act.wait_ge(pe_up, 2 * NM * b + 2 * m + 1)
                if not (first(b) and m < 3):
                    act.wait_ge(dve_hid, NM * b + m - 2)
                sc.activation(silu[:, m % 3, :], ps[:, W1_BANKS[m], :], ACT.Silu).then_inc(act_silu, 1)

            def qk1_out(b):
                act.wait_ge(pe_x2, 4 * b + 2)
                sc.activation(q1[:], ps[:, 6, :], ACT.Copy).then_inc(act_qk1, 1)
                act.wait_ge(pe_x2, 4 * b + 3)
                sc.activation(k1a[:], ps[:, 5, :], ACT.Copy).then_inc(act_qk1, 1)

            def exp1(b, n):
                t0, nt = GROUPS1[n]
                act.wait_ge(dve_m1, NB1 * b + n + 1)
                if n == 2:
                    act.wait_ge(pe_pT, NB1 * b + 1)
                col = 0
                for t in range(t0, t0 + nt):
                    w = (t + 1) * P
                    last = sc.activation(prob1[n][:, col:col + w], ps[:, bank1(b, n), col:col + w], ACT.Exp,
                                         bias=nmax1[:, 1, t:t + 1], scale=SCALE1,
                                         accum_out=den1[:, 0, t:t + 1])
                    col += w
                last.then_inc(act_p1, 1)

            def x3_out(b):
                act.wait_ge(pe_x3, 1 * b + 1)
                sc.activation(x3_hi[:], ps[:, 6, :], ACT.Copy).then_inc(act_x3, 1)

            def hidden1_out(b, f):
                act.wait_ge(pe_h1, NF * b + f + 1)
                sc.activation(actT[:, f, :], ps[:, 5 + f % 2, :], ACT.Identity, bias=fb1_c[:, f:f + 1])
                sc.activation(ang[:, f, :], ps[:, 5 + f % 2, :], ACT.Identity, bias=th[:, 0, f:f + 1],
                              scale=0.1 / TWO_PI).then_inc(act_h1, 1)

            def sines(b, f):
                act.wait_ge(dve_ang, NF * b + f + 1)
                sc.activation(ang[:, f, :], ang[:, f, :], ACT.Sin, scale=TURN).then_inc(act_sin, 1)

            def rectify(b, f):
                act.wait_ge(dve_act, NF * b + f + 1)
                sc.activation(actT[:, f, :], actT[:, f, :], ACT.Relu).then_inc(act_relu, 1)

            xT_out(0)
            act.wait_ge(w_dve, 1)
            for a in range(2):
                for which in range(2):
                    part(0, which, a)
            act.wait_ge(w_dve, W_TURNS)
            sc.activation(th[:, 4:6, :], th[:, 2:4, :], ACT.Sin, scale=TURN).then_inc(w_act, 1)
            act.wait_ge(w_up_in, 32)
            for n, hi in enumerate(up_hi):
                for dst, src in tiles_of(hi, stage[:, n]):
                    sc.activation(dst, src, ACT.Copy).then_inc(w_hi, 1)
            act.wait_ge(w_in, 16 * N_SMALL)
            sc.activation(f1_hi[:], f1[:], ACT.Copy).then_inc(w_hi, 1)
            load_table(ACT.Exp, 1)

            def element(b, more, back):
                prev = b - 1
                for n in range(NQ):
                    exps(b, n)
                    if back and n == X1[1]:
                        qk1_out(prev)
                    for k in range(NB1):
                        if back and A1[k] == n:
                            exp1(prev, k)
                if more:
                    xT_out(b + 1)
                    part(b + 1, 0, 0)
                    part(b + 1, 1, 0)
                zT_out(b)
                load_table(ACT.Silu, 0)
                if back:
                    x3_out(prev)
                if back:
                    hidden1_out(prev, 0)
                    hidden1_out(prev, 1)
                x1_hi_out(b)
                if more:
                    part(b + 1, 0, 1)
                    part(b + 1, 1, 1)
                x1T_out(b)
                if back:
                    hidden1_out(prev, 2)
                    hidden1_out(prev, 3)
                for m in range(NM):
                    if more and m in (1, 2):
                        act.wait_ge(dve_qk, 2 * b + 2 + m)
                    silus(b, m)
                    if back and m == SIN_AT:
                        for f in range(NF):
                            sines(prev, f)
                    if back and 6 <= m < 10:
                        rectify(prev, m - 6)
                    if m == 6:
                        gate_tanh(b)
                load_table(ACT.Exp, 1)

            element(0, True, False)
            with act.Fori(1, B - 1) as b:
                element(b, True, True)
            element(B - 1, False, True)
            last = B - 1
            qk1_out(last)
            for n in range(NB1):
                exp1(last, n)
            x3_out(last)
            load_table(ACT.Sin, 0)
            for f in range(NF):
                hidden1_out(last, f)
                if f >= 2:
                    sines(last, f - 2)
            sines(last, 2)
            rectify(last, 0)
            sines(last, 3)
            for f in range(1, NF):
                rectify(last, f)

        @block.tensor
        def _(pe):
            mm, tr = nc.tensor.matmul, nc.tensor.transpose

            def split3(dst, hi, lo, vhi, vlo):
                mm(dst, hi, vhi, start=True, stop=False)
                mm(dst, hi, vlo, start=False, stop=False)
                return mm(dst, lo, vhi, start=False, stop=True)

            def cols(t):
                return slice(t * P, (t + 1) * P)

            def project(b):
                pe.wait_ge(x_in, 16 * b + 16)
                for t in range(NT):
                    last = tr(ps[:, 0, cols(t)], xin[:, t, :], ident[:])
                last.then_inc(pe_proj, 1)

            def project_qk(b):
                pe.wait_ge(act_xT, 1 * b + 1)
                mm(ps[:, 1, :], wq0[:], xT, start=True, stop=True).then_inc(pe_proj, 1)
                mm(ps[0:KV, 2, :], wk0[:], xT, start=True, stop=True).then_inc(pe_proj, 1)

            def project_v(b):
                for t in range(NT):
                    last = mm(ps[:, 3, KV * t:KV * (t + 1)], xT[:, cols(t)], wv0[:], start=True, stop=True)
                last.then_inc(pe_proj, 1)

            def keep_clock(n, bank):
                for _ in range(n):
                    mm(ps[:, bank, 0:P], ident[:], ident[:], start=True, stop=True)

            def scores_for_max(b, j):
                qt, h0, hn = MAX_GROUPS[j]
                n, pair = (qt + 1) * P, 2 * (j % 2)
                if j == 0:
                    pe.wait_ge(qk_in, 16 * (PARTS + 1) * (b + 1))
                if j >= 2:
                    pe.wait_ge(dve_max, NG * b + j - 1)
                elif not first(b):
                    pe.wait_ge(dve_hid, NM * b - 1 + j)
                for k in range(2 * hn):
                    dst = ps[:, pair + k // hn, k % hn * n:(k % hn + 1) * n]
                    mm(dst, qstack[0:ROWS, h0 + k, cols(qt)], kstack[0:ROWS, (h0 + k) % H, 0:n],
                       start=True, stop=False)
                    last = mm(dst[:, qt * P:n], ident_h[:], future_h[:, 0, :], start=False, stop=True)
                last.then_inc(pe_max, 1)

            def transpose_max(b):
                pe.wait_ge(dve_max, NG * (b + 1))
                for t in range(NT):
                    last = tr(ps[0:NH, 0, cols(t)], negmax[:, t, :], ident[:])
                last.then_inc(pe_mrow, 1)

            def exact_unit(b, n):
                g, u = n // NU, n % NU
                pair = 2 * (n % 2)
                if n == 0:
                    pe.wait_ge(m_in, 16 * PARTS * (b + 1))
                if n >= 2:
                    pe.wait_ge(act_exp, NQ * b + n - 1)
                for kb, h, col, q0 in UNITS[u]:
                    n_q = S - q0
                    last = mm(ps[:, pair + col // 512, col % 512:col % 512 + n_q], kstack[:, h, cols(kb)],
                              qstack[:, H * g + h, q0:S], start=True, stop=True)
                last.then_inc(pe_unit, 1)

            def values(b, g, k):
                bank = (7, 4)[g % 2]
                if k == 0:
                    pe.wait_ge(pool_mask, NQ * b + NU * g + H)
                    if g == 0:
                        pe.wait_ge(dve_part, 3 * b + 3)
                    elif g >= 2:
                        pe.wait_ge(dve_uT, G * b + g - 1)
                elif k == 2:
                    pe.wait_ge(pool_mask, NQ * b + NU * (g + 1))
                for kb in ((0,), (1, 3), (2,))[k]:
                    for h in range(H):
                        u, col, q0 = PLACE[kb, h]
                        last = mm(ps[32 * h:32 * h + 32, bank, q0:S], vext[:, kb, h, :],
                                  probs[:, g % 2, u, col:col + S - q0], start=(kb == 0), stop=(kb == 2))
                if k == 2:
                    last.then_inc(pe_av, 1)

            def transpose_o(b, t):
                if t == 0:
                    pe.wait_ge(dve_uT, G * (b + 1))
                if t >= 2:
                    pe.wait_ge(dve_o, NT * b + t - 1)
                for g in range(G):
                    last = tr(ps[:, (7, 4)[t % 2], cols(g)], uT[:, g, cols(t)], ident[:])
                last.then_inc(pe_o, 1)

            def transpose_z(b):
                pe.wait_ge(dve_z, 1 * b + 1)
                for t in range(NT):
                    last = tr(ps[:, 7, cols(t)], attn[:, t, :], ident[:])
                last.then_inc(pe_tail, 1)

            def project_out(b):
                pe.wait_ge(act_zT, 1 * b + 1)
                for t in range(NT):
                    last = mm(ps[:, 4, cols(t)], zT[:, cols(t)], wo0[:], start=True, stop=True)
                last.then_inc(pe_tail, 1)

            def transpose_x1(b):
                pe.wait_ge(dve_x1, 1 * b + 1)
                for t in range(NT):
                    last = tr(ps[:, 7, cols(t)], x1[:, t, :], ident[:])
                last.then_inc(pe_tail, 1)

            def gate(b):
                pe.wait_ge(act_x1T, 2 * b + 2)
                for t in range(NT):
                    last = mm(ps[:, 4, E * t:E * (t + 1)], x1T[:, cols(t)], gateT, start=True, stop=True)
                last.then_inc(pe_tail, 1)

            def experts_up(b, m, more, back):
                if m == 0:
                    pe.wait_ge(dve_x1lo, 1 * b + 1)
                if W1_BEFORE[m] is not None:
                    pe.wait_ge(act_silu, NM * b + W1_BEFORE[m] + 1)
                elif m == 1 and more:
                    pe.wait_ge(dve_part, 3 * b + 5)
                elif m == 3:
                    pe.wait_ge(dve_lg, 2 * b + 1)
                split3(ps[:, W1_BANKS[m], :], up_hi[0][:, m, :], up_lo[0][:, m, :],
                       x1_hi[:], x1_lo[:]).then_inc(pe_up, 1)
                if W3_BEFORE[m] is not None:
                    pe.wait_ge(dve_hid, NM * b + W3_BEFORE[m] + 1)
                elif m < 2 and more:
                    pe.wait_ge(dve_part, 3 * b + (4, 6)[m])
                elif m >= 2 and back:
                    pe.wait_ge(act_h1, NF * b)
                split3(ps[:, W3_BANKS[m], :], up_hi[1][:, m, :], up_lo[1][:, m, :],
                       x1_hi[:], x1_lo[:]).then_inc(pe_up, 1)

            def experts_down(b, n):
                t, e, half = n // (2 * E), n // 2 % E, n % 2
                if n == 0:
                    pe.wait_ge(dve_hid, NM * (b + 1))
                for j in ((0, 1, 2), (3, 4, 5))[half]:
                    last = mm(ps[:, DOWN_BANKS[t], cols(e)], hidT[:, EXPERT_TILES[e][j], cols(t)],
                              down[:, e * (FULL + 1) + j, :], start=(e == 0 and j == 0),
                              stop=(j == FULL), skip_group_check=True)
                if e == E - 1 and half:
                    last.then_inc(pe_down, 1)

            def project1(b, k):
                if k == 0:
                    pe.wait_ge(dve_x2, 1 * b + 1)
                    for t in range(NT):
                        last = tr(ps[:, 5, cols(t)], x2[:, t, :], ident[:])
                    last.then_inc(pe_x2, 1)
                elif k == 1:
                    pe.wait_ge(dve_x2T, 1 * b + 1)
                    for bank, w in ((6, wq1), (5, wk1)):
                        mm(ps[:, bank, :], w[:].rearrange("p a d -> p (a d)"), x2T[:], start=True,
                           stop=True).then_inc(pe_x2, 1)
                else:
                    pe.wait_ge(dve_q1, 1 * b + 1)
                    for t in range(NT):
                        last = mm(ps[:, 6, cols(t)], x2T[:, cols(t)], wv1[:], start=True, stop=True)
                    last.then_inc(pe_x2, 1)

            def scores1(b, n):
                t0, nt = GROUPS1[n]
                if n == 0:
                    pe.wait_ge(dve_k1, 1 * b + 1)
                elif n == 1:
                    pe.wait_ge(dve_v1, 1 * b + 1)
                elif not final(b):
                    pe.wait_ge(dve_r3, NB1 * b + 1)
                col = 0
                for t in range(t0, t0 + nt):
                    w = (t + 1) * P
                    dst = ps[:, bank1(b, n), col:col + w]
                    mm(dst, q1[:, cols(t)], k1a[:, 0:w], start=True, stop=False)
                    mm(dst, q1[:, cols(t)], k1b[:, 0:w], start=False, stop=False)
                    last = mm(dst[:, t * P:w], ident_h[:], future_h[:, 0, :], start=False, stop=True)
                    col += w
                last.then_inc(pe_s1, 1)

            def transpose_p1(b, n):
                t0, nt = GROUPS1[n]
                pe.wait_ge(act_p1, NB1 * b + n + 1)
                for k in range(sum(t + 1 for t in range(t0, t0 + nt))):
                    last = tr(ps[:, bank1(b, n), cols(k)], prob1[n][:, cols(k)], ident[:])
                last.then_inc(pe_pT, 1)

            def values1(b, n):
                t0, nt = GROUPS1[n]
                pe.wait_ge(dve_pT, NB1 * b + n + 1)
                k = 0
                for t in range(t0, t0 + nt):
                    for kb in range(t + 1):
                        last = mm(ps[:, bank1(b, n), cols(t - t0)], probT1[n][:, cols(k)], v1[:, kb, :],
                                  start=(kb == 0), stop=(kb == t))
                        k += 1
                last.then_inc(pe_av1, 1)

            def transpose_x3(b):
                pe.wait_ge(dve_x3, 1 * b + 1)
                for t in range(NT):
                    last = tr(ps[:, 6, cols(t)], x3[:, t, :], ident[:])
                last.then_inc(pe_x3, 1)

            def hidden1(b, f):
                if f == 0:
                    pe.wait_ge(dve_x3lo, 1 * b + 1)
                if f >= 2:
                    pe.wait_ge(act_h1, NF * b + f - 1)
                split3(ps[:, 5 + f % 2, :], f1_hi[:, cols(f)], f1_lo[:, cols(f)],
                       x3_hi[:], x3_lo[:]).then_inc(pe_h1, 1)

            def output1(b, f):
                if f == 0:
                    pe.wait_ge(act_h1, NF * b + 3)
                pe.wait_ge(act_relu, NF * b + f + 1)
                for t in range(NT):
                    last = mm(ps[:, 5, cols(t)], actT[:, f, cols(t)], f2[:, f, :], start=(f == 0 and t == 0),
                              stop=(f == NF - 1), skip_group_check=True)
                if f == NF - 1:
                    last.then_inc(pe_y, 1)

            pe.wait_ge(w_pool, Z_CONST)
            pe.wait_ge(w_first, 16 * N_FIRST)
            tr(ps[:, 5, 0:N_VEC], vec_rows[:], ident[0:N_VEC, 0:N_VEC]).then_inc(w_pe, 1)
            project(0)
            project_qk(0)
            project_v(0)
            pe.wait_ge(w_in, 16 * N_SMALL)

            def element(b, more, back):
                prev = b - 1
                for j in range(NG):
                    scores_for_max(b, j)
                    if back and j < DOWN_EARLY:
                        experts_down(prev, j)
                    elif not back:
                        keep_clock(2, 7)
                transpose_max(b)
                if back:
                    for n in range(DOWN_EARLY, DOWN_PIECES):
                        experts_down(prev, n)
                for n in range(NQ):
                    exact_unit(b, n)
                    for step, at in ((project1, X1), (scores1, S1), (transpose_p1, T1), (values1, V1)):
                        for k in range(len(at)):
                            if back and at[k] == n:
                                step(prev, k)
                    if n > NU and 1 <= n % NU <= 3:
                        values(b, n // NU - 1, n % NU - 1)
                values(b, G - 1, 0)
                if back:
                    values1(prev, NB1 - 1)
                values(b, G - 1, 1)
                values(b, G - 1, 2)
                for t in range(NT):
                    transpose_o(b, t)
                if more:
                    project(b + 1)
                    project_qk(b + 1)
                keep_clock(FILL[0], 0)
                transpose_z(b)
                keep_clock(FILL[1], 0)
                project_out(b)
                if back:
                    transpose_x3(prev)
                if more:
                    project_v(b + 1)
                if back:
                    for f in range(3):
                        hidden1(prev, f)
                keep_clock(FILL[2 if back else 4], 0)
                transpose_x1(b)
                if back:
                    hidden1(prev, 3)
                keep_clock(FILL[3], 0)
                if first(b):
                    pe.wait_ge(w_lo, 7)
                for m in range(NM):
                    experts_up(b, m, more, back)
                    if m == 1:
                        gate(b)
                    if back and 9 <= m < 13:
                        output1(prev, m - 9)
                if first(b):
                    pe.wait_ge(w_down_in, 16 * 2 * E)

            element(0, True, False)
            with pe.Fori(1, B - 1) as b:
                element(b, True, True)
            element(B - 1, False, True)
            for n in range(DOWN_PIECES):
                experts_down(B - 1, n)
            keep_clock(TAIL_FILL[0], 1)
            for k in range(3):
                project1(B - 1, k)
                keep_clock(TAIL_FILL[1 + k], 1)
            for n, step in enumerate((scores1, transpose_p1, values1)):
                for k in range(NB1):
                    step(B - 1, k)
                keep_clock(TAIL_FILL[4 + n], 1)
            transpose_x3(B - 1)
            keep_clock(TAIL_FILL[7], 1)
            for f in range(NF):
                hidden1(B - 1, f)
            keep_clock(TAIL_FILL[8], 1)
            for f in range(NF):
                output1(B - 1, f)

        @block.vector
        def _(dve):
            ve = nc.vector
            front = Chain(dve, ch0, N_FRONT)
            back = Chain(dve, ch1, N_BACK)

            def layer_norm(chain, n, src, dst, done, stages=range(LN_STAGES), tiles=range(NT)):
                var, root, r, g = (ln_s[n][:, i, :] for i in range(4))
                for k in stages:
                    if k > 0:
                        chain.wait()
                    if k == 0:
                        for t in tiles:
                            last = ve.bn_stats(stats[n][:, t, :], src[:, t, :])
                        chain.mark(last)
                    elif k == 1:
                        ve.memset(r[:, 0:1], 0.0)
                        for t in range(NT):
                            last = ve.bn_aggr(mv[n][:, t, :], stats[n][:, t, :])
                        chain.mark(last)
                    elif k == 2:
                        chain.mark(ve.tensor_scalar(var, mv[n][:, :, 1], EPS, None, ALU.add))
                    elif k == 3:
                        chain.mark(ve.tensor_scalar(root.bitcast(I32), var.bitcast(I32), -0.5, RSQRT_SEED,
                                                    ALU.mult, ALU.add))
                    elif k == 4:
                        chain.mark(ve.scalar_tensor_tensor(g, root, -0.5, var, ALU.mult, ALU.mult))
                    elif k < LN_STAGES - 1:
                        if k % 2:
                            ins = ve.tensor_tensor(r, g, root, ALU.mult)
                        else:
                            if k < LN_STAGES - 2:
                                ve.scalar_tensor_tensor(g, r, 1.5, g, ALU.add, ALU.mult)
                            ins = ve.scalar_tensor_tensor(root, r, 1.5, root, ALU.add, ALU.mult)
                        chain.mark(ins)
                    else:
                        for t in range(NT):
                            last = ve.tensor_scalar(dst[:, t, :], src[:, t, :], mv[n][:, t, 0:1],
                                                    root[:, t:t + 1], ALU.subtract, ALU.mult)
                        last.then_inc(done, 1)

            def part_rest(b, which, a):
                dst, src, bias = ((qparts, ps[:, 1, :], bq_c), (kparts, ps[0:KV, 2, :], bk_c[0:KV]))[which]
                work = rest[which]
                dve.wait_ge(act_part, 4 * b + 2 * a - 1 + which)
                if a == 1:
                    ve.scalar_tensor_tensor(work, src, bias, dst[:, 0, :], ALU.add,
                                            ALU.subtract).then_inc(dve_part, 1)
                else:
                    ve.tensor_tensor(dst[:, 2, :], work, dst[:, 1, :], ALU.subtract).then_inc(dve_qk, 1)

            def values_in(b):
                dve.wait_ge(pe_proj, 4 * b + 4)
                if not first(b):
                    dve.wait_ge(pe_av, G * b)
                ve.tensor_tensor(vext[:, :, :, 0:HD],
                                 ps[:, 3, 0:NT * KV].rearrange("p (t h d) -> p t h d", t=NT, h=H),
                                 bv_r[:].rearrange("p (a h d) -> p a h d", a=1, h=H).to_broadcast([P, NT, H, HD]),
                                 ALU.add).then_inc(dve_part, 1)

            def maxima(b, j):
                qt, h0, hn = MAX_GROUPS[j]
                n = (qt + 1) * P
                dve.wait_ge(pe_max, NG * b + j + 1)
                if j == 0 and not first(b):
                    dve.wait_ge(pe_mrow, 1 * b)
                pair = 2 * (j % 2)
                ve.tensor_reduce(negmax[:, qt, h0:h0 + 2 * hn].rearrange("p (a h) -> p a h", a=2),
                                 ps[:, pair:pair + 2, 0:hn * n].rearrange("p a (h n) -> p a h n", h=hn),
                                 axis=AX.X, op=ALU.max, negate=True).then_inc(dve_max, 1)

            def max_parts(b):
                dve.wait_ge(pe_mrow, 1 * b + 1)
                if not first(b):
                    dve.wait_ge(m_in, 16 * PARTS * b)
                front.link(ve.tensor_copy(mparts[:, 0, :], ps[0:NH, 0, :]))
                ve.tensor_tensor(mrow[:], ps[0:NH, 0, :], mparts[:, 0, :], ALU.subtract).then_inc(dve_mrow, 1)
                dve.wait_ge(dve_mrow, 2 * b + 1)
                front.link(ve.tensor_copy(mparts[:, 1, :], mrow[:]))
                ve.tensor_tensor(mparts[:, 2, :], mrow[:], mparts[:, 1, :], ALU.subtract).then_inc(dve_mrow, 1)

            def uT_out(b, g):
                dve.wait_ge(pe_av, G * b + g + 1)
                ve.tensor_copy(uT[:, g, :], ps[:, (7, 4)[g % 2], :]).then_inc(dve_uT, 1)

            def divide(b, t):
                dve.wait_ge(pe_o, NT * b + t + 1)
                if t == 0 and not first(b):
                    dve.wait_ge(dve_z, 1 * b)
                heads = ps[:, (7, 4)[t % 2], :].rearrange("p (h c) -> p h c", c=32)
                front.mark(ve.reciprocal(rden0[:, t, :], heads[:, :, HD]))
                if t:
                    dve.wait_ge(dve_o, NT * b + t)
                    ve.bn_stats(stats[0][:, t - 1, :], att[:, t - 1, :])
                front.wait()
                ve.tensor_tensor(att[:, t, :].rearrange("p (h c) -> p h c", c=HD), heads[:, :, 0:HD],
                                 rden0[:, t, :].unsqueeze(2).to_broadcast([P, NH, HD]),
                                 ALU.mult).then_inc(dve_o, 1)

            def norm_z(b, k):
                if k == 0:
                    dve.wait_ge(dve_o, NT * (b + 1))
                    if not first(b):
                        dve.wait_ge(pe_tail, 4 * b)
                layer_norm(front, 0, att, attn, dve_z, (k,), (NT - 1,))

            def norm_x1(b, k):
                if k == 0:
                    dve.wait_ge(pe_tail, 4 * b + 2)
                    dve.wait_ge(x_res, 1 * b + 1)
                    ve.tensor_tensor(res1[:].rearrange("p t d -> p (t d)"), ps[:, 4, :],
                                     xres[:].rearrange("p t d -> p (t d)"), ALU.add).then_inc(dve_wo, 1)
                    dve.wait_ge(dve_wo, 1 * b + 1)
                    if not first(b):
                        dve.wait_ge(dve_y2, 2 * b)
                layer_norm(front, 0, res1, x1, dve_x1, (k,))

            def x1_lower(b):
                dve.wait_ge(act_x1T, 2 * b + 1)
                ve.tensor_tensor(x1_lo[:], ps[:, 7, :], x1_hi[:].bitcast(FP32), ALU.subtract).then_inc(dve_x1lo, 1)

            def gate_choice(b, k):
                other = lg[:].unsqueeze(2).to_broadcast([P, NT, E, E])
                own = lg[:].unsqueeze(3).to_broadcast([P, NT, E, E])
                if k == 0:
                    dve.wait_ge(pe_tail, 4 * b + 4)
                    ve.tensor_copy(lg[:].rearrange("p t e -> p (t e)"), ps[:, 4, 0:NT * E]).then_inc(dve_lg, 1)
                elif k == 1:
                    dve.wait_ge(dve_lg, 2 * b + 1)
                    ve.tensor_tensor(cmp4[:, 0], other, own, ALU.is_gt)
                    front.mark(ve.tensor_tensor(cmp4[:, 1], other, own, ALU.is_equal))
                else:
                    front.wait()
                if k == 2:
                    front.mark(ve.tensor_tensor(cmp4[:, 1].rearrange("p t e j -> p t (e j)"),
                                                cmp4[:, 1].rearrange("p t e j -> p t (e j)"),
                                                before[:].rearrange("p e j -> p (e j)").unsqueeze(1)
                                                .to_broadcast([P, NT, E * E]), ALU.mult))
                elif k == 3:
                    front.mark(ve.tensor_tensor(cmp4[:, 0], cmp4[:, 0], cmp4[:, 1], ALU.add))
                elif k == 4:
                    front.mark(ve.tensor_reduce(lgx[:, 0], cmp4[:, 0], axis=AX.X, op=ALU.add))
                elif k == 5:
                    front.mark(ve.tensor_scalar(lgx[:, 0], lgx[:, 0], 2.0, 0.5, ALU.is_lt, ALU.mult))
                elif k == 6:
                    front.mark(ve.tensor_tensor(lgx[:, 1], lgx[:, 0], lg[:], ALU.mult))
                elif k == 7:
                    front.mark(ve.tensor_reduce(lgs[:], lgx[:, 1], axis=AX.X, op=ALU.add))
                elif k == 8:
                    ve.tensor_tensor(lgx[:, 2], lg[:], lgs[:].unsqueeze(2).to_broadcast([P, NT, E]),
                                     ALU.subtract).then_inc(dve_lg, 1)

            def gate_weights(b):
                dve.wait_ge(act_gate, 1 * b + 1)
                ve.scalar_tensor_tensor(cw[:], lgx[:, 3], 1.0, lgx[:, 0], ALU.add, ALU.mult).then_inc(dve_cw, 1)

            def expert_hidden(b, m):
                dve.wait_ge(act_silu, NM * b + m + 1)
                dve.wait_ge(pe_up, 2 * NM * b + 2 * m + 2)
                if m == 0:
                    dve.wait_ge(pe_av, G * (b + 1))
                ve.tensor_tensor(hidT[:, m, :], silu[:, m % 3, :], ps[:, W3_BANKS[m], :],
                                 ALU.mult).then_inc(dve_hid, 1)

            def mix(b, tiles):
                if 0 in tiles:
                    back.begin(b)
                    dve.wait_ge(dve_cw, 1 * b + 1)
                for e in range(E):
                    for t in tiles:
                        if e == 0:
                            dve.wait_ge(pe_down, NT * b + t + 1)
                        src = x1 if e == 0 else res
                        ins = ve.scalar_tensor_tensor(res[:, t, :], ps[:, DOWN_BANKS[t], e * D:(e + 1) * D],
                                                      cw[:, t, e:e + 1], src[:, t, :], ALU.mult, ALU.add)
                    if e < E - 1:
                        back.link(ins)
                ins.then_inc(dve_y2, 1)

            def norm_x2(b):
                mix(b, range(NT - 1))
                dve.wait_ge(dve_y2, 2 * b + 1)
                for t in range(NT - 1):
                    ve.bn_stats(stats[1][:, t, :], res[:, t, :])
                mix(b, (NT - 1,))
                dve.wait_ge(dve_y2, 2 * (b + 1))
                layer_norm(back, 1, res, x2, dve_x2, tiles=(NT - 1,))

            def x2T_out(b):
                dve.wait_ge(pe_x2, 4 * b + 1)
                ve.tensor_copy(x2T[:], ps[:, 5, :]).then_inc(dve_x2T, 1)

            def v1_out(b):
                dve.wait_ge(pe_x2, 4 * b + 4)
                ve.tensor_copy(four[:, 1, :], ps[:, 6, :]).then_inc(dve_v1, 1)

            def qk_halves1(b):
                dve.wait_ge(act_qk1, 2 * b + 1)
                ve.tensor_tensor(q1[64:P, :], ps[64:P, 6, :], q1[64:P, :].bitcast(FP32),
                                 ALU.subtract).then_inc(dve_q1, 1)
                dve.wait_ge(act_qk1, 2 * b + 2)
                ve.tensor_copy(k1b[64:P, :], ps[64:P, 5, :])
                back.link(ve.tensor_tensor(k1b[0:64, :], ps[0:64, 5, :], k1a[0:64, :].bitcast(FP32),
                                           ALU.subtract))
                ve.tensor_tensor(k1a[64:P, :], ps[64:P, 5, :], k1a[64:P, :].bitcast(FP32),
                                 ALU.subtract).then_inc(dve_k1, 1)

            def maximum1(b, n):
                t0, nt = GROUPS1[n]
                dve.wait_ge(pe_s1, NB1 * b + n + 1)
                col = 0
                for t in range(t0, t0 + nt):
                    w = (t + 1) * P
                    last = ve.tensor_reduce(nmax1[:, 0, t:t + 1], ps[:, bank1(b, n), col:col + w], axis=AX.X,
                                            op=ALU.max, negate=True)
                    col += w
                back.link(last)
                ve.tensor_scalar(nmax1[:, 1, t0:t0 + nt], nmax1[:, 0, t0:t0 + nt], SCALE1, None,
                                 ALU.mult).then_inc(dve_m1, 1)

            def probs_out1(b, n):
                t0, nt = GROUPS1[n]
                dve.wait_ge(pe_pT, NB1 * b + n + 1)
                if n == 2:
                    dve.wait_ge(pe_av1, NB1 * b + 1)
                w = P * sum(t + 1 for t in range(t0, t0 + nt))
                ve.tensor_copy(probT1[n][:, 0:w], ps[:, bank1(b, n), 0:w]).then_inc(dve_pT, 1)

            def attend1(b, n):
                t0, nt = GROUPS1[n]
                dve.wait_ge(act_p1, NB1 * b + n + 1)
                back.link(ve.reciprocal(den1[:, 1, t0:t0 + nt], den1[:, 0, t0:t0 + nt]))
                dve.wait_ge(pe_av1, NB1 * b + n + 1)
                for t in range(t0, t0 + nt):
                    last = ve.scalar_tensor_tensor(res[:, t, :], ps[:, bank1(b, n), (t - t0) * D:(t - t0 + 1) * D],
                                                   den1[:, 1, t:t + 1], x2[:, t, :], ALU.mult, ALU.add)
                last.then_inc(dve_r3, 1)

            def norm_x3(b, k):
                if k == 0:
                    dve.wait_ge(dve_r3, NB1 * (b + 1))
                layer_norm(back, 1, res, x3, dve_x3, (k,))

            def x3_lower(b):
                dve.wait_ge(act_x3, 1 * b + 1)
                ve.tensor_tensor(x3_lo[:], ps[:, 6, :], x3_hi[:].bitcast(FP32), ALU.subtract).then_inc(dve_x3lo, 1)

            def angle(b, f, k):
                a = ang[:, f, :]
                if k == 0:
                    dve.wait_ge(act_h1, NF * b + f + 1)
                    if f:
                        dve.wait_ge(dve_ang, NF * b + f)
                    back.mark(ve.tensor_scalar(ang_n[:], a, ROUND, ROUND, ALU.add, ALU.subtract))
                else:
                    back.wait()
                    ve.tensor_tensor(a, a, ang_n[:], ALU.subtract).then_inc(dve_ang, 1)

            def activate(b, f):
                dve.wait_ge(act_sin, NF * b + f + 1)
                ve.scalar_tensor_tensor(actT[:, f, :], ang[:, f, :], th[:, 1, f:f + 1],
                                        actT[:, f, :], ALU.mult, ALU.add).then_inc(dve_act, 1)

            def norm_out(b, k):
                if k == 0:
                    dve.wait_ge(pe_y, 1 * b + 1)
                    dve.wait_ge(pool_x3, 1 * b + 1)
                    back.link(ve.tensor_tensor(res[:].rearrange("p t d -> p (t d)"), ps[:, 5, :],
                                               x3[:].rearrange("p t d -> p (t d)"), ALU.add))
                    dve.wait_ge(y_out, 16 * b + 1)
                layer_norm(back, 1, res, y, dve_y, (k,))
                if k == LN_STAGES - 1:
                    back.end()

            def prepare():
                k = [1]

                def step(ins):
                    k[0] += 1
                    ins.then_inc(w_dve, 1)
                    dve.wait_ge(w_dve, k[0])

                step(ve.tensor_scalar(th[:, 6, :], theta_c, 1.0 / TWO_PI, None, ALU.mult))
                step(ve.tensor_scalar(th[:, 6, :], th[:, 6, :], ROUND, ROUND, ALU.add, ALU.subtract))
                step(ve.scalar_tensor_tensor(th[:, 7, :], th[:, 6, :], -PI_C1, theta_c, ALU.mult, ALU.add))
                step(ve.scalar_tensor_tensor(th[:, 7, :], th[:, 6, :], -PI_C2, th[:, 7, :], ALU.mult, ALU.add))
                step(ve.tensor_scalar(th[:, 7, :], th[:, 7, :], 1.0 / TWO_PI, 0.5, ALU.mult, ALU.min))
                step(ve.tensor_scalar(th[:, 2, :], th[:, 7, :], -0.5, None, ALU.max))
                step(ve.tensor_scalar(th[:, 7, :], th[:, 2, :], 0.25, None, ALU.add))
                step(ve.tensor_scalar(th[:, 6, :], th[:, 7, :], ROUND, ROUND, ALU.add, ALU.subtract))
                step(ve.tensor_tensor(th[:, 3, :], th[:, 7, :], th[:, 6, :], ALU.subtract))
                assert k[0] == W_TURNS
                dve.wait_ge(w_act, 1)
                step(ve.tensor_tensor(th[:, 6, :], th[:, 5, :], w_real_c, ALU.mult))
                step(ve.tensor_tensor(th[:, 7, :], th[:, 4, :], w_imag_c, ALU.mult))
                step(ve.tensor_tensor(th[:, 6, :], th[:, 6, :], th[:, 7, :], ALU.add))
                step(ve.scalar_tensor_tensor(th[:, 0, :], fb1_c, 0.1 / TWO_PI, th[:, 2, :], ALU.mult, ALU.add))
                step(ve.scalar_tensor_tensor(th[:, 1, :], th[:, 6, :], 0.1, w_imag_c, ALU.mult, ALU.mult))

            ve.memset(qstack[64:P].rearrange("p h n -> p (h n)").bitcast(FP32), 0.0)
            ve.memset(kstack[64:P].rearrange("p h n -> p (h n)").bitcast(FP32), 0.0).then_inc(w_zero, 1)
            dve.wait_ge(w_first, 16 * N_FIRST)
            dve.wait_ge(w_pe, 1)
            ve.tensor_copy(vecs[:], ps[:, 5, 0:N_VEC]).then_inc(w_dve, 1)
            dve.wait_ge(w_dve, 1)
            part_rest(0, 0, 1)
            part_rest(0, 1, 1)
            part_rest(0, 0, 2)
            values_in(0)
            part_rest(0, 1, 2)
            prepare()

            def element(b, more, has_back):
                prev = b - 1
                front.begin(b)
                for j in range(NG):
                    maxima(b, j)
                max_parts(b)
                if has_back:
                    norm_x2(prev)
                    x2T_out(prev)
                    qk_halves1(prev)
                uT_out(b, 0)
                if has_back:
                    v1_out(prev)
                    maximum1(prev, 0)
                    maximum1(prev, 1)
                    probs_out1(prev, 0)
                    probs_out1(prev, 1)
                uT_out(b, 1)
                if has_back:
                    attend1(prev, 0)
                    attend1(prev, 1)
                    maximum1(prev, 2)
                    probs_out1(prev, 2)
                uT_out(b, 2)
                if has_back:
                    attend1(prev, 2)
                    norm_x3(prev, 0)
                uT_out(b, 3)
                if has_back:
                    for k in range(1, X3_EARLY):
                        norm_x3(prev, k)
                for t in range(NT):
                    divide(b, t)
                for k in range(LN_STAGES):
                    norm_z(b, k)
                if has_back:
                    for k in range(X3_EARLY, LN_STAGES):
                        norm_x3(prev, k)
                for k in range(LN_STAGES):
                    norm_x1(b, k)
                    if has_back and k == 0:
                        x3_lower(prev)
                if more:
                    part_rest(b + 1, 0, 1)
                    part_rest(b + 1, 1, 1)
                x1_lower(b)
                if more:
                    values_in(b + 1)
                    part_rest(b + 1, 0, 2)
                    part_rest(b + 1, 1, 2)
                if has_back:
                    for f in (0, 1):
                        angle(prev, f, 0)
                        angle(prev, f, 1)
                for m in range(NM):
                    expert_hidden(b, m)
                    if m == 0:
                        gate_choice(b, 0)
                    if has_back and m < 2:
                        angle(prev, m + 2, 0)
                        angle(prev, m + 2, 1)
                    if has_back and 3 <= m < 7:
                        activate(prev, m - 3)
                    if 2 <= m < 6:
                        for k in (2 * m - 3, 2 * m - 2):
                            gate_choice(b, k)
                    if m == 7:
                        gate_weights(b)
                        front.end()
                    if has_back and OUT_AT <= m < OUT_AT + LN_STAGES // 2:
                        norm_out(prev, 2 * (m - OUT_AT))
                        norm_out(prev, 2 * (m - OUT_AT) + 1)

            element(0, True, False)
            with dve.Fori(1, B - 1) as b:
                element(b, True, True)
            element(B - 1, False, True)
            last_b = B - 1
            norm_x2(last_b)
            x2T_out(last_b)
            qk_halves1(last_b)
            v1_out(last_b)
            for step in (maximum1, probs_out1, attend1):
                for n in range(NB1):
                    step(last_b, n)
            for k in range(LN_STAGES):
                norm_x3(last_b, k)
            x3_lower(last_b)
            for f in range(NF):
                for k in range(2):
                    angle(last_b, f, k)
                if f >= 2:
                    activate(last_b, f - 2)
            activate(last_b, 2)
            activate(last_b, 3)
            for k in range(LN_STAGES):
                norm_out(last_b, k)


_INS = ['L0_attn_x', 'L0_attn_Wq', 'L0_attn_bq', 'L0_attn_Wk', 'L0_attn_bk', 'L0_attn_Wv', 'L0_attn_bv',
        'L0_attn_ln_g', 'L0_attn_ln_b', 'L0_attn_Wo', 'L0_attn_bo', 'L0_ffn_gate_w', 'L0_ffn_w1', 'L0_ffn_w2',
        'L0_ffn_w3', 'L1_attn_Wq', 'L1_attn_Wk', 'L1_attn_Wv', 'L1_ffn_W1', 'L1_ffn_b1',
        'L1_ffn_quantum_phases', 'L1_ffn_quantum_weights_real', 'L1_ffn_quantum_weights_imag', 'L1_ffn_W2',
        'L1_ffn_b2']


def kernel(**inputs):
    import concourse.bacc as _bacc
    from concourse.bass_utils import run_bass_kernel_spmd as _run

    nc = _bacc.Bacc("TRN2", target_bir_lowering=False, num_devices=1)
    arrays, args = {}, []
    for name in _INS:
        a = np.ascontiguousarray(inputs[name])
        arrays[f"in_{name}"] = a
        args.append(nc.dram_tensor(f"in_{name}", a.shape, mybir.dt.from_np(a.dtype), kind="ExternalInput").ap())
    args.append(nc.dram_tensor("out_0", (B, S, D), FP32, kind="ExternalOutput").ap())
    build(nc, *args)
    r = _run(nc, [arrays], core_ids=[0])
    return r.results[0]["out_0"]
```
